# Optimizing a Trainium2 kernel written in Bass

```python
import numpy as np
import jax
import jax.numpy as jnp

def _softmax(x, axis=-1):
    return jax.nn.softmax(x, axis=axis)

def _gelu(x):
    return jax.nn.gelu(x, approximate=True)

def _silu(x):
    return jax.nn.silu(x)

def _sigmoid(x):
    return jax.nn.sigmoid(x)

def _layernorm(x, axis=-1, eps=1e-05):
    m = jnp.mean(x, axis=axis, keepdims=True)
    v = jnp.var(x, axis=axis, keepdims=True)
    return (x - m) / jnp.sqrt(v + eps)

def _scatter_add(tgt, idx, src, axis=0):
    return tgt.at[idx].add(src)

def _segment_sum(src, seg, n):
    return jax.ops.segment_sum(src, seg, n)
kernel_name = 'mk_recurrent_d2_jaxref_r8_5a699d'

def setup_inputs(seed: int=0):
    np.random.seed(seed)
    _w = jnp.asarray

    def _L0_attn_setup():
        import math
        import jax, jax.numpy as jnp
        import numpy as np
        B, T, D = (2, 256, 256)
        NH, NKV = (32, 8)
        HD = D // NH
        key = jax.random.key(seed)
        kx, kq, kk, kv, ko = jax.random.split(key, 5)
        s = 1.0 / math.sqrt(D)
        return {'x': jax.random.normal(kx, (B, T, D), dtype=jnp.float32), 'wq': jax.random.normal(kq, (D, NH * HD), dtype=jnp.float32) * s, 'wk': jax.random.normal(kk, (D, NKV * HD), dtype=jnp.float32) * s, 'wv': jax.random.normal(kv, (D, NKV * HD), dtype=jnp.float32) * s, 'wo': jax.random.normal(ko, (NH * HD, D), dtype=jnp.float32) * s}
    _L0_attn_in = _L0_attn_setup()

    def _L0_ffn_setup():
        import jax, jax.numpy as jnp
        import numpy as np
        NUM_EXPERTS = 32
        TOP_K = 4
        HIDDEN = 256
        INTER = 96
        key = jax.random.key(seed)
        k1, k2, k3, k4 = jax.random.split(key, 4)
        hidden_states = jax.random.normal(k1, (4, 64, HIDDEN), dtype=jnp.float32)
        gate = jax.random.normal(k2, (HIDDEN, NUM_EXPERTS), dtype=jnp.float32) * 0.02
        gate_up_proj = jax.random.normal(k3, (NUM_EXPERTS, HIDDEN, 2 * INTER), dtype=jnp.float32) * 0.02
        down_proj = jax.random.normal(k4, (NUM_EXPERTS, INTER, HIDDEN), dtype=jnp.float32) * 0.02
        return {'hidden_states': hidden_states, 'gate': gate, 'gate_up_proj': gate_up_proj, 'down_proj': down_proj}
    _L0_ffn_in = _L0_ffn_setup()

    def _L1_attn_setup():
        import jax, jax.numpy as jnp
        import numpy as np
        NV, NK, DK, DV, KC = (32, 16, 128, 128, 4)
        EPS = 1e-06

        def _silu(x):
            return x * jax.nn.sigmoid(x)

        def _l2norm(x):
            return x * jax.lax.rsqrt(jnp.sum(x * x, axis=-1, keepdims=True) + EPS)

        def _gated_delta_rule(q, k, v, g, beta):
            tm = lambda x: jnp.moveaxis(x, 1, 0)
            B, T, H = (q.shape[0], q.shape[1], q.shape[2])
            S0 = jnp.zeros((B, H, q.shape[-1], v.shape[-1]), q.dtype)

            def step(S, xs):
                qt, kt, vt, gt, bt = xs
                S = S * jnp.exp(gt)[..., None, None]
                kS = jnp.einsum('bhk,bhkv->bhv', kt, S)
                S = S + bt[..., None, None] * kt[..., :, None] * (vt - kS)[..., None, :]
                o = jnp.einsum('bhk,bhkv->bhv', qt, S)
                return (S, o)
            _, o = jax.lax.scan(step, S0, (tm(q), tm(k), tm(v), tm(g), tm(beta)))
            return jnp.moveaxis(o, 0, 1)
        key = jax.random.key(seed)
        ks = jax.random.split(key, 10)
        B, T, D = (2, 512, 256)
        key_dim, value_dim = (NK * DK, NV * DV)
        conv_dim = 2 * key_dim + value_dim
        s = 0.02
        return {'hidden_states': jax.random.normal(ks[0], (B, T, D), jnp.float32), 'W_qkv': jax.random.normal(ks[1], (D, conv_dim), jnp.float32) * s, 'W_z': jax.random.normal(ks[2], (D, value_dim), jnp.float32) * s, 'W_b': jax.random.normal(ks[3], (D, NV), jnp.float32) * s, 'W_a': jax.random.normal(ks[4], (D, NV), jnp.float32) * s, 'conv_w': jax.random.normal(ks[5], (conv_dim, KC), jnp.float32) * 0.2, 'dt_bias': jnp.ones((NV,), jnp.float32), 'A_log': jnp.log(jax.random.uniform(ks[6], (NV,), jnp.float32, 0.5, 16.0)), 'norm_w': jnp.ones((DV,), jnp.float32), 'W_out': jax.random.normal(ks[7], (value_dim, D), jnp.float32) * s}
    _L1_attn_in = _L1_attn_setup()

    def _L1_ffn_setup():
        import jax, jax.numpy as jnp
        import numpy as np
        H = 256
        I = 176
        E = 8
        K = 2
        B, S = (2, 256)
        key = jax.random.key(seed)
        k0, k1, k2, k3, k4 = jax.random.split(key, 5)
        scale = 1.0 / np.sqrt(H)
        x = jax.random.normal(k0, (B, S, H), dtype=jnp.float32)
        Wr = jax.random.normal(k1, (H, E), dtype=jnp.float32) * scale
        Wg = jax.random.normal(k2, (E, H, I), dtype=jnp.float32) * scale
        Wu = jax.random.normal(k3, (E, H, I), dtype=jnp.float32) * scale
        Wd = jax.random.normal(k4, (E, I, H), dtype=jnp.float32) * (1.0 / np.sqrt(I))
        return {'x': x, 'Wr': Wr, 'Wg': Wg, 'Wu': Wu, 'Wd': Wd}
    _L1_ffn_in = _L1_ffn_setup()
    _d = {'L0_attn_x': _L0_attn_in['x'], 'L0_attn_wq': _L0_attn_in['wq'], 'L0_attn_wk': _L0_attn_in['wk'], 'L0_attn_wv': _L0_attn_in['wv'], 'L0_attn_wo': _L0_attn_in['wo'], 'L0_ffn_gate': _L0_ffn_in['gate'], 'L0_ffn_gate_up_proj': _L0_ffn_in['gate_up_proj'], 'L0_ffn_down_proj': _L0_ffn_in['down_proj'], 'L1_attn_W_qkv': _L1_attn_in['W_qkv'], 'L1_attn_W_z': _L1_attn_in['W_z'], 'L1_attn_W_b': _L1_attn_in['W_b'], 'L1_attn_W_a': _L1_attn_in['W_a'], 'L1_attn_conv_w': _L1_attn_in['conv_w'], 'L1_attn_dt_bias': _L1_attn_in['dt_bias'], 'L1_attn_A_log': _L1_attn_in['A_log'], 'L1_attn_norm_w': _L1_attn_in['norm_w'], 'L1_attn_W_out': _L1_attn_in['W_out'], 'L1_ffn_Wr': _L1_ffn_in['Wr'], 'L1_ffn_Wg': _L1_ffn_in['Wg'], 'L1_ffn_Wu': _L1_ffn_in['Wu'], 'L1_ffn_Wd': _L1_ffn_in['Wd']}
    _x0 = _d['L0_attn_x']
    _d['L0_attn_x'] = jax.random.normal(jax.random.fold_in(jax.random.key(seed), 1), (1, 1024, 256), dtype=_x0.dtype)
    del _x0
    return _d

def reference(L0_attn_x, L0_attn_wq, L0_attn_wk, L0_attn_wv, L0_attn_wo, L0_ffn_gate, L0_ffn_gate_up_proj, L0_ffn_down_proj, L1_attn_W_qkv, L1_attn_W_z, L1_attn_W_b, L1_attn_W_a, L1_attn_conv_w, L1_attn_dt_bias, L1_attn_A_log, L1_attn_norm_w, L1_attn_W_out, L1_ffn_Wr, L1_ffn_Wg, L1_ffn_Wu, L1_ffn_Wd):

    def _L0_attn_ref(x, wq, wk, wv, wo):
        import math
        import jax, jax.numpy as jnp
        import numpy as np
        B, T, D = (2, 256, 256)
        NH, NKV = (32, 8)
        HD = D // NH
        bsz, seqlen, _ = x.shape
        q = (x @ wq).reshape(bsz, seqlen, NH, HD).transpose(0, 2, 1, 3)
        k = (x @ wk).reshape(bsz, seqlen, NKV, HD).transpose(0, 2, 1, 3)
        v = (x @ wv).reshape(bsz, seqlen, NKV, HD).transpose(0, 2, 1, 3)
        rep = NH // NKV
        k = jnp.repeat(k, rep, axis=1)
        v = jnp.repeat(v, rep, axis=1)
        att = jnp.einsum('bhqd,bhkd->bhqk', q.astype(jnp.float32), k.astype(jnp.float32)) / math.sqrt(HD)
        mask = jnp.triu(jnp.ones((seqlen, seqlen), dtype=bool), k=1)
        att = jnp.where(mask[None, None, :, :], -jnp.inf, att)
        att = jax.nn.softmax(att, axis=-1)
        y = jnp.einsum('bhqk,bhkd->bhqd', att, v.astype(jnp.float32)).astype(q.dtype)
        y = y.transpose(0, 2, 1, 3).reshape(bsz, seqlen, NH * HD)
        return y @ wo

    def _L0_ffn_ref(hidden_states, gate, gate_up_proj, down_proj):
        import jax, jax.numpy as jnp
        import numpy as np
        NUM_EXPERTS = 32
        TOP_K = 4
        HIDDEN = 256
        INTER = 96
        batch_size = hidden_states.shape[0]
        x = hidden_states.reshape(-1, HIDDEN)
        num_tokens = x.shape[0]
        router_logits = jnp.einsum('TD,DE->TE', x, gate)
        routing_weights = jax.nn.softmax(router_logits.astype(jnp.float32), axis=-1)
        top_k_weights, top_k_indices = jax.lax.top_k(routing_weights, TOP_K)
        top_k_weights = top_k_weights / top_k_weights.sum(axis=-1, keepdims=True)
        top_k_weights = top_k_weights.astype(x.dtype)
        router_weights = jnp.zeros((num_tokens, NUM_EXPERTS), dtype=x.dtype)
        token_indices = jnp.broadcast_to(jnp.arange(num_tokens)[:, None], top_k_indices.shape)
        router_weights = router_weights.at[token_indices, top_k_indices].set(top_k_weights)
        gate_up = jnp.einsum('TD,EDF->TEF', x, gate_up_proj)
        g, u = jnp.split(gate_up, 2, axis=-1)
        gated = u * jax.nn.silu(g)
        next_states = jnp.einsum('TEF,EFD->TED', gated, down_proj)
        next_states = (next_states * router_weights[..., None]).sum(axis=1)
        return next_states.reshape(batch_size, -1, HIDDEN)

    def _L1_attn_ref(hidden_states, W_qkv, W_z, W_b, W_a, conv_w, dt_bias, A_log, norm_w, W_out):
        import jax, jax.numpy as jnp
        import numpy as np
        NV, NK, DK, DV, KC = (32, 16, 128, 128, 4)
        EPS = 1e-06

        def _silu(x):
            return x * jax.nn.sigmoid(x)

        def _l2norm(x):
            return x * jax.lax.rsqrt(jnp.sum(x * x, axis=-1, keepdims=True) + EPS)

        def _gated_delta_rule(q, k, v, g, beta):
            tm = lambda x: jnp.moveaxis(x, 1, 0)
            B, T, H = (q.shape[0], q.shape[1], q.shape[2])
            S0 = jnp.zeros((B, H, q.shape[-1], v.shape[-1]), q.dtype)

            def step(S, xs):
                qt, kt, vt, gt, bt = xs
                S = S * jnp.exp(gt)[..., None, None]
                kS = jnp.einsum('bhk,bhkv->bhv', kt, S)
                S = S + bt[..., None, None] * kt[..., :, None] * (vt - kS)[..., None, :]
                o = jnp.einsum('bhk,bhkv->bhv', qt, S)
                return (S, o)
            _, o = jax.lax.scan(step, S0, (tm(q), tm(k), tm(v), tm(g), tm(beta)))
            return jnp.moveaxis(o, 0, 1)
        B, T, D = hidden_states.shape
        key_dim, value_dim = (NK * DK, NV * DV)
        mixed = hidden_states @ W_qkv
        z = (hidden_states @ W_z).reshape(B, T, NV, DV)
        beta = jax.nn.sigmoid(hidden_states @ W_b)
        a = hidden_states @ W_a
        g = -jnp.exp(A_log) * jax.nn.softplus(a + dt_bias)
        xp = jnp.pad(mixed, ((0, 0), (KC - 1, 0), (0, 0)))
        conv = sum((xp[:, i:i + T, :] * conv_w[:, i] for i in range(KC)))
        mixed = _silu(conv)
        q, k, v = jnp.split(mixed, [key_dim, 2 * key_dim], axis=-1)
        q = q.reshape(B, T, NK, DK)
        k = k.reshape(B, T, NK, DK)
        v = v.reshape(B, T, NV, DV)
        rep = NV // NK
        q = jnp.repeat(q, rep, axis=2)
        k = jnp.repeat(k, rep, axis=2)
        q = _l2norm(q) * DK ** (-0.5)
        k = _l2norm(k)
        o = _gated_delta_rule(q, k, v, g, beta)
        var = jnp.mean(o * o, axis=-1, keepdims=True)
        o = o * jax.lax.rsqrt(var + 1e-06) * norm_w * _silu(z)
        return o.reshape(B, T, value_dim) @ W_out

    def _L1_ffn_ref(x, Wr, Wg, Wu, Wd):
        import jax, jax.numpy as jnp
        import numpy as np
        H = 256
        I = 176
        E = 8
        K = 2
        B, S = (2, 256)
        router_logits = jnp.einsum('bsh,he->bse', x, Wr)
        probs = jax.nn.softmax(router_logits.astype(jnp.float32), axis=-1)
        topk_w, topk_idx = jax.lax.top_k(probs, K)
        topk_w = topk_w / jnp.sum(topk_w, axis=-1, keepdims=True)
        onehot = jax.nn.one_hot(topk_idx, E, dtype=topk_w.dtype)
        combine = jnp.einsum('bsk,bske->bse', topk_w, onehot)
        g = jnp.einsum('bsh,ehi->besi', x, Wg)
        u = jnp.einsum('bsh,ehi->besi', x, Wu)
        h = jax.nn.silu(g) * u
        y = jnp.einsum('besi,eih->besh', h, Wd)
        out = jnp.einsum('bse,besh->bsh', combine.astype(x.dtype), y)
        return out
    x = L0_attn_x
    xn = _layernorm(x, axis=-1)
    s = _L0_attn_ref(xn, L0_attn_wq, L0_attn_wk, L0_attn_wv, L0_attn_wo)
    g = _silu(_L0_ffn_ref(xn, L0_ffn_gate, L0_ffn_gate_up_proj, L0_ffn_down_proj))
    x = x + s * g
    xn = _layernorm(x, axis=-1)
    s = _L1_attn_ref(xn, L1_attn_W_qkv, L1_attn_W_z, L1_attn_W_b, L1_attn_W_a, L1_attn_conv_w, L1_attn_dt_bias, L1_attn_A_log, L1_attn_norm_w, L1_attn_W_out)
    g = _silu(_L1_ffn_ref(xn, L1_ffn_Wr, L1_ffn_Wg, L1_ffn_Wu, L1_ffn_Wd))
    x = x + s * g
    return x

_drawn_inputs = setup_inputs


def setup_inputs(seed=0):
    import zlib

    import numpy as np

    out = dict(_drawn_inputs(seed))
    spreads = {'L1_attn_dt_bias': (1.0, 0.6), 'L1_attn_norm_w': (1.0, 0.6)}
    factors = {'L0_attn_wq': 8.0,
     'L0_attn_wk': 8.0,
     'L0_attn_wv': 8.0,
     'L0_attn_wo': 8.0,
     'L0_ffn_gate': 8.0,
     'L0_ffn_gate_up_proj': 8.0,
     'L0_ffn_down_proj': 8.0,
     'L1_attn_W_qkv': 4.528,
     'L1_attn_W_z': 4.567,
     'L1_attn_W_b': 8.0,
     'L1_attn_W_a': 8.0,
     'L1_attn_conv_w': 4.551,
     'L1_attn_A_log': 8.0,
     'L1_attn_W_out': 4.544,
     'L1_ffn_Wr': 5.241,
     'L1_ffn_Wg': 4.948,
     'L1_ffn_Wu': 4.63,
     'L1_ffn_Wd': 4.614}
    for name, (base, spread) in spreads.items():
        noise = np.random.default_rng([zlib.crc32(name.encode()), seed]).standard_normal(out[name].shape)
        drawn = base * np.exp(spread * noise) if base else spread * noise
        out[name] = jnp.asarray(drawn.astype(out[name].dtype))
    for name, factor in factors.items():
        out[name] = (out[name] * factor).astype(out[name].dtype)
    return out
```

```python
from contextlib import ExitStack

import numpy as np

import concourse.bass as bass
from concourse import mybir

ALU = mybir.AluOpType
ACT = mybir.ActivationFunctionType
AX = mybir.AxisListType
F32 = mybir.dt.float32
BF16 = mybir.dt.bfloat16
I32 = mybir.dt.int32

P = 128
T, D = 1024, 256
NC = T // P
KT = D // P
HALF = 512
NH, NKV, HD = 32, 8, 8
REP = NH // NKV
E0, TOP0, F0 = 32, 4, 96
G0 = 4
TILES0 = G0 * F0 // P
E1, TOP1, F1 = 8, 2, 176
TILES1 = E1 * F1 // P
ESEL = 32
NV, NK, DK = 32, 16, 128
TAPS = 4
LEVELS = 7
UNITS = 2 * NC
NEG = -1e30
PAIRS = [(0, 0), (0, 1), (1, 0), (1, 1), (0, 2), (2, 0)]
QROWS = HD * len(PAIRS)
SCALE = float(HD) ** -0.5
LN_EPS = 1e-5


class Memory:
    pass


class Chain:

    def __init__(self, eng, sem, base=0):
        self.eng, self.sem, self.base, self.n = eng, sem, base, 0

    def __call__(self, instruction):
        instruction.then_inc(self.sem, 1)
        self.n += 1

    def wait(self):
        self.eng.wait_ge(self.sem, self.base + self.n)

    def link(self, instruction):
        self(instruction)
        self.wait()


def dve_layer_norm(dve, step, x, st, mv, xn, s_var, s_rstd, rstd):
    for c in range(NC):
        step(dve.bn_stats(st[:, c, :], x[:, c, :]))
    step.wait()
    for c in range(NC):
        last = dve.bn_aggr(mv[:, c, :], st[:, c, :])
    last.then_inc(s_var, 1)
    dve.wait_ge(s_var, 1)
    dve.wait_ge(s_rstd, 1)
    for c in range(NC):
        step(dve.tensor_scalar(xn[:, c, :], x[:, c, :], mv[:, c, 0:1], rstd[:, c:c + 1],
                               ALU.subtract, ALU.mult))


def pool_rsqrt_var(nc, pool, step, mv, rstd, minus_half, s_var, s_rstd):
    pool.wait_ge(s_var, 1)
    step.link(nc.gpsimd.tensor_scalar(rstd[:, 0:NC], mv[:, :, 1], LN_EPS, None, ALU.add))
    nc.gpsimd.tensor_tensor(rstd[:, 0:NC], rstd[:, 0:NC], minus_half[:, 0:1].broadcast_to([P, NC]),
                            ALU.pow).then_inc(s_rstd, 1)


def pool_expert_rows(nc, step, sel, width, experts):
    for part in range(3):
        ap = sel[ESEL * part:ESEL * part + ESEL, :]
        step.link(nc.gpsimd.affine_select(out=ap, in_=ap, compare_op=ALU.is_ge, fill=0.0, base=0,
                                          pattern=[[1, experts * width]], channel_multiplier=-width))
        step.link(nc.gpsimd.affine_select(out=ap, in_=ap, compare_op=ALU.is_ge, fill=0.0, base=width - 1,
                                          pattern=[[-1, experts * width]], channel_multiplier=width))


def dve_route(dve, step, logits, n_exp, k, rev, w, b, s_logit, s_exp, w3b, w3f):
    lg, pr, left, pick, acc = w
    r1, ix = b
    all_e = [P, NC, n_exp]

    def col(ap):
        return ap[:, :].unsqueeze(2).broadcast_to(all_e)

    step.link(dve.tensor_reduce(r1[:, :], logits, AX.X, ALU.max))
    dve.tensor_tensor(lg[:, :, 0:n_exp], logits, col(r1), ALU.subtract).then_inc(s_logit, 1)
    dve.wait_ge(s_exp, 1)
    step.link(dve.tensor_reduce(r1[:, :], pr[:, :, 0:n_exp], AX.X, ALU.add))
    step.link(dve.reciprocal(r1[:, :], r1[:, :]))
    step.link(dve.tensor_tensor(pr[:, :, 0:n_exp], pr[:, :, 0:n_exp], col(r1), ALU.mult))
    step.link(dve.tensor_copy(left[:, :, 0:n_exp], pr[:, :, 0:n_exp]))
    for n in range(k):
        step.link(dve.tensor_reduce(r1[:, :], left[:, :, 0:n_exp], AX.X, ALU.max))
        step.link(dve.tensor_tensor(pick[:, :, 0:n_exp], left[:, :, 0:n_exp], col(r1), ALU.is_equal))
        step.link(dve.tensor_tensor(pick[:, :, 0:n_exp], pick[:, :, 0:n_exp],
                                    rev[:, 0:n_exp].unsqueeze(1).broadcast_to(all_e), ALU.mult))
        step.link(dve.tensor_reduce(ix[:, :], pick[:, :, 0:n_exp], AX.X, ALU.max))
        step.link(dve.tensor_tensor(pick[:, :, 0:n_exp], pick[:, :, 0:n_exp], col(ix), ALU.is_equal))
        step.link(dve.scalar_tensor_tensor(out=left[:, :, 0:n_exp], in0=pick[:, :, 0:n_exp], scalar=-4.0,
                                           in1=left[:, :, 0:n_exp], op0=ALU.mult, op1=ALU.add))
    step.link(dve.tensor_scalar(pick[:, :, 0:n_exp], left[:, :, 0:n_exp], 0.0, None, ALU.is_lt))
    step.link(dve.tensor_tensor(acc[:, :, 0:n_exp], pick[:, :, 0:n_exp], pr[:, :, 0:n_exp], ALU.mult))
    step.link(dve.tensor_reduce(r1[:, :], acc[:, :, 0:n_exp], AX.X, ALU.add))
    step.link(dve.reciprocal(r1[:, :], r1[:, :]))
    step.link(dve.tensor_tensor(acc[:, :, 0:n_exp], acc[:, :, 0:n_exp], col(r1), ALU.mult))
    for part in range(3):
        at = slice(ESEL * part, ESEL * part + n_exp)
        step.link(dve.tensor_copy(w3b[:, :, at], acc[:, :, 0:n_exp]))
        step.link(dve.tensor_copy(w3f[:, :, at], w3b[:, :, at]))
        if part < 2:
            step.link(dve.tensor_tensor(acc[:, :, 0:n_exp], acc[:, :, 0:n_exp], w3f[:, :, at], ALU.subtract))


def build(nc, x, w_attn, w_o, gate0, gu0, down0, w_conv, w_tap, w_z, w_out, w_ba, dt_bias, a_log, norm_w,
          router1, gu1, down1, out):
    with ExitStack() as ctx:
        m = Memory()

        def sb(name, shape, dt=F32):
            return ctx.enter_context(nc.sbuf_tensor(name, shape, dt))

        m.ps = ctx.enter_context(nc.psum_tensor("ps", [P, 8, HALF], F32))
        m.x = sb("x_nat", [P, NC, D])
        m.xn = sb("xn_nat", [P, NC, D])
        m.xnT = sb("xnT", [P, KT, T])
        m.ident = sb("ident", [P, P])
        m.identb = sb("identb", [P, P], BF16)
        m.upto = sb("upto", [P, P])
        m.after = sb("after", [P, P])
        m.ones = sb("ones", [P, P])
        m.future = sb("future", [P, P], BF16)
        m.lmask = sb("lmask", [P, LEVELS, P // 2])
        m.pair_mask = sb("pair_mask", [P, P // 2, 2])
        m.minus_half = sb("minus_half", [P, 1])
        m.plus_half = sb("plus_half", [P, 1])
        m.rev = sb("rev", [P, E0])
        m.yacc = sb("yacc", [P, NC, D])
        m.st = sb("bn_st", [P, NC, 6])
        m.mv = sb("bn_mv", [P, NC, 2])
        m.rstd = sb("rstd", [P, NC])

        with ExitStack() as l0:
            def sb0(name, shape, dt=F32):
                return l0.enter_context(nc.sbuf_tensor(name, shape, dt))
            m.sel0 = sb0("sel0", [P, E0 * F0], BF16)
            m.wT3 = sb0("wT3", [P, T], BF16)
            m.qst = sb0("q_stack", [P, NH, T], BF16)
            m.kst = sb0("k_stack", [P, NKV, T], BF16)
            m.vaug = sb0("v_aug", [P, NKV, NC, 32])
            m.w_o = sb0("w_o", [P, KT, D])
            m.mpart = sb0("m_part", [P, NC, NH, 2])
            stage_inputs(nc, m, x, w_attn, w_o, gate0)
            stage_moe0_and_maxima(nc, m, gu0, down0)
            stage_attention(nc, m)
        m.beta = sb("beta", [P, NV, NC])
        m.g = sb("g", [P, NV + 2, NC])
        m.eg = sb("decays", [P, 3, NV, NC])
        m.neg_egc = sb("neg_egc", [P, NV, NC])
        m.taps = sb("taps", [P, NK + 1, 4, TAPS])
        m.norm_w = sb("norm_w_half", [P, 1])
        with ExitStack() as l1:
            m.sel1 = l1.enter_context(nc.sbuf_tensor("sel1", [P, E1 * F1], BF16))
            m.wT3 = l1.enter_context(nc.sbuf_tensor("l1_wT3", [P, T], BF16))
            stage_l1_inputs(nc, m, router1, w_ba, dt_bias, a_log, norm_w, w_tap)
            stage_moe1(nc, m, gu1, down1)
        stage_delta(nc, m, w_conv, w_z, w_out, out)
        stage_store(nc, m, out)


def stage_inputs(nc, m, x, w_attn, w_o, gate0):
    with ExitStack() as ctx:
        def sb(name, shape, dt=F32):
            return ctx.enter_context(nc.sbuf_tensor(name, shape, dt))

        def sem(name):
            return ctx.enter_context(nc.semaphore(name))

        ps = m.ps
        NQ, NKC = NH * HD, NKV * HD
        wa = sb("w_attn_sb", [P, KT, NQ + 2 * NKC + E0])
        qp = sb("q_parts", [P, 3, KT, T], BF16)
        kp = sb("k_parts", [NKC, 3, T], BF16)
        rest = sb("rest", [P, 2, T])
        irev = sb("irev", [P, E0], I32)
        route = [sb(f"route{i}", [P, NC, E0]) for i in range(5)]
        route_col = [sb(f"route_col{i}", [P, NC]) for i in range(2)]
        w3b = sb("w3b", [P, NC, 3 * ESEL], BF16)
        w3f = sb("w3f", [P, NC, 3 * ESEL])
        scratch_q = nc.dram_tensor("scratch_q", [3, NQ, T], BF16).ap()
        scratch_k = nc.dram_tensor("scratch_k", [3, NKC, T], BF16).ap()
        in_x, in_w, in_wo = sem("in_x"), sem("in_w"), sem("in_wo")
        s_const, s_ident = sem("const_made"), sem("ident_made")
        s_var, s_rstd, s_xn, s_tr, s_xnT = sem("var"), sem("rstd"), sem("xn_made"), sem("xn_transposed"), sem("xnT_made")
        s_proj = sem("projected")
        s_parts = sem("parts_split")
        s_stored, s_stacked, s_zero = sem("parts_stored"), sem("stacks_loaded"), sem("stacks_zeroed")
        s_dve, s_pool = sem("dve_steps"), sem("pool_steps")
        s_logit, s_exp = sem("logits_shifted"), sem("exp_made")
        s_w3zero = sem("w3_zeroed")
        s_w3, s_wt, s_wT3 = sem("w3_split"), sem("w3_transposed"), sem("wT3_made")
        block = ctx.enter_context(nc.Block())

        @block.sync
        def _(sp):
            sp.dma_start(m.x[:], x.rearrange("b (c p) d -> p (b c) d", p=P)).then_inc(in_x, 16)
            sp.dma_start(wa[:, :, 0:NQ + 2 * NKC], w_attn.rearrange("(k p) n -> p k n", p=P)).then_inc(in_w, 16)
            sp.dma_start(wa[:, :, NQ + 2 * NKC:], gate0.rearrange("(k p) n -> p k n", p=P)).then_inc(in_w, 16)
            sp.dma_start(m.w_o[:], w_o.rearrange("(k p) n -> p k n", p=P)).then_inc(in_wo, 16)
            sp.wait_ge(s_parts, 3)
            sp.dma_start(scratch_k.rearrange("s c t -> c s t"), kp[:]).then_inc(s_stored, 16)
            for k in range(KT):
                for part in range(3):
                    sp.dma_start(scratch_q[part, k * P:(k + 1) * P, :], qp[:, part, k, :]).then_inc(s_stored, 16)
            sp.wait_ge(s_stored, 16 * 7)
            sp.wait_ge(s_zero, 2)
            for r, (a, b) in enumerate(PAIRS):
                rows = slice(HD * r, HD * (r + 1))
                sp.dma_start(m.qst[rows, :, :], scratch_q[a].rearrange("(h d) t -> d h t", d=HD)).then_inc(s_stacked, 16)
                sp.dma_start(m.kst[rows, :, :], scratch_k[b].rearrange("(h d) t -> d h t", d=HD)).then_inc(s_stacked, 16)
            sp.wait_ge(s_stacked, 32 * len(PAIRS))
            sp.wait_ge(in_wo, 16)

        @block.gpsimd
        def _(pool):
            step = Chain(pool, s_pool)
            g = nc.gpsimd

            def select(ap, op, base, pattern, cm, fill):
                step.link(g.affine_select(out=ap, in_=ap, compare_op=op, fill=fill, base=base,
                                          pattern=pattern, channel_multiplier=cm))
            step(g.memset(m.minus_half[:], -0.5))
            step(g.memset(m.plus_half[:], 0.5))
            step.link(g.memset(m.ident[:], 0.0))
            select(m.ident[:], ALU.not_equal, 0, [[-1, P]], 1, 1.0)
            g.tensor_copy(m.identb[:], m.ident[:]).then_inc(s_ident, 1)
            pool_rsqrt_var(nc, pool, step, m.mv, m.rstd, m.minus_half, s_var, s_rstd)
            step(g.memset(m.mpart[:], NEG))
            step(g.iota(irev[:], pattern=[[-1, E0]], base=E0, channel_multiplier=0))
            step(g.memset(m.upto[:], 1.0))
            step(g.memset(m.after[:], 1.0))
            step(g.memset(m.ones[:], 1.0))
            step(g.memset(m.future[:], 0.0))
            step(g.memset(m.lmask[:], 1.0))
            step(g.memset(m.pair_mask[:], 0.0))
            step(g.memset(m.sel0[:], 1.0))
            step.wait()
            step(g.tensor_copy(m.rev[:], irev[:]))
            step.link(g.memset(m.kst[:], 0.0))
            step.link(g.memset(m.kst[32:64, :, :], 1.0))
            select(m.kst[32:64, :, :], ALU.is_ge, QROWS + 2 - 32, [[0, NKV], [0, T]], -1, 0.0)
            pool.sem_inc(s_zero, 1)
            g.memset(w3f[:], 0.0).then_inc(s_w3zero, 1)
            select(m.upto[:], ALU.is_ge, 0, [[1, P]], -1, 0.0)
            select(m.after[:], ALU.is_ge, -1, [[-1, P]], 1, 0.0)
            select(m.future[:], ALU.is_ge, 0, [[1, P]], -1, NEG)
            select(m.pair_mask[:, :, 1], ALU.not_equal, 0, [[-2, P // 2]], 1, -1.0)
            for lv in range(LEVELS):
                s = 1 << lv
                ap = m.lmask[:, lv, :].rearrange("p (b s) -> p b s", s=s)
                select(ap, ALU.is_ge, -s, [[-2 * s, P // (2 * s)], [0, s]], 1, 0.0)
                select(ap, ALU.is_ge, 2 * s - 1, [[2 * s, P // (2 * s)], [0, s]], -1, 0.0)
            pool_expert_rows(nc, step, m.sel0, F0, E0)

        @block.vector
        def _(dve):
            step = Chain(dve, s_dve)
            dve.wait_ge(in_x, 16)
            dve_layer_norm(dve, step, m.x, m.st, m.mv, m.xn, s_var, s_rstd, m.rstd)
            step.wait()
            dve.memset(m.qst[:], 0.0).then_inc(s_zero, 1)
            step.link(dve.memset(m.vaug[:], 0.0))
            step.link(dve.memset(m.vaug[:, :, :, HD:HD + 1], 1.0))
            for n in range(3):
                dve.wait_ge(s_proj, n + 1)
                rows = P if n < 2 else NKC
                banks = slice(4 + 2 * n, 6 + 2 * n) if n < 2 else slice(0, 2)
                src = ps[0:rows, banks, :].rearrange("p b n -> p (b n)")
                parts = [qp[:, s, n, :] if n < 2 else kp[:, s, :] for s in range(3)]
                step.link(dve.tensor_copy(parts[0], src))
                step.link(dve.tensor_tensor(rest[0:rows, 0, :], src, parts[0], ALU.subtract))
                step.link(dve.tensor_copy(parts[1], rest[0:rows, 0, :]))
                dve.tensor_tensor(parts[2], rest[0:rows, 0, :], parts[1], ALU.subtract).then_inc(s_parts, 1)
                dve.wait_ge(s_parts, n + 1)
            dve.wait_ge(s_proj, 4)
            step(dve.tensor_copy(m.vaug[:, :, :, 0:HD].rearrange("p g c d -> p c g d"),
                                 ps[:, 2, :].rearrange("p (c g d) -> p c g d", c=NC, d=HD)))
            dve.wait_ge(s_proj, 5)
            dve.wait_ge(s_w3zero, 1)
            dve_route(dve, step, ps[:, 3, 0:NC * E0].rearrange("p (c e) -> p c e", e=E0), E0, TOP0, m.rev,
                      route, route_col, s_logit, s_exp, w3b, w3f)
            dve.sem_inc(s_w3, 1)

        @block.tensor
        def _(pe):
            pe.wait_ge(s_ident, 1)
            pe.wait_ge(s_dve, 2 * NC)
            for k in range(KT):
                for c in range(NC):
                    mm = pe.transpose(ps[:, 2 * k + c // 4, (c % 4) * P:(c % 4 + 1) * P],
                                      m.xn[:, c, k * P:(k + 1) * P], m.ident[:])
                mm.then_inc(s_tr, 1)
            pe.wait_ge(in_w, 32)
            pe.wait_ge(s_xnT, 2)
            for n in range(2):
                for h in range(2):
                    for k in range(KT):
                        mm = pe.matmul(ps[:, 4 + 2 * n + h, :], wa[:, k, n * P:(n + 1) * P],
                                       m.xnT[:, k, h * HALF:(h + 1) * HALF], start=k == 0, stop=k == KT - 1)
                mm.then_inc(s_proj, 1)
            for h in range(2):
                for k in range(KT):
                    mm = pe.matmul(ps[0:NKC, h, :], wa[:, k, NQ:NQ + NKC],
                                   m.xnT[:, k, h * HALF:(h + 1) * HALF], start=k == 0, stop=k == KT - 1)
            mm.then_inc(s_proj, 1)
            for bank, a, n in ((2, NQ + NKC, NKC), (3, NQ + 2 * NKC, E0)):
                for c in range(NC):
                    for k in range(KT):
                        mm = pe.matmul(ps[:, bank, c * n:(c + 1) * n], m.xnT[:, k, c * P:(c + 1) * P],
                                       wa[:, k, a:a + n], start=k == 0, stop=k == KT - 1)
                mm.then_inc(s_proj, 1)
            pe.wait_ge(s_w3, 1)
            pe.wait_ge(s_parts, 3)
            for c in range(NC):
                mm = pe.transpose(ps[0:3 * ESEL, c // 4, (c % 4) * P:(c % 4 + 1) * P], w3f[:, c, :], m.ident[:])
            mm.then_inc(s_wt, 1)

        @block.scalar
        def _(act):
            for k in range(KT):
                act.wait_ge(s_tr, k + 1)
                nc.scalar.copy(m.xnT[:, k, :], ps[:, 2 * k:2 * k + 2, :].rearrange("p b n -> p (b n)")).then_inc(s_xnT, 1)
            act.wait_ge(s_logit, 1)
            nc.scalar.activation(route[1][:], route[0][:], ACT.Exp).then_inc(s_exp, 1)
            act.wait_ge(s_wt, 1)
            nc.scalar.copy(m.wT3[0:3 * ESEL, :], ps[0:3 * ESEL, 0:2, :].rearrange("p b n -> p (b n)")).then_inc(s_wT3, 1)
            act.wait_ge(s_wT3, 1)


def moe_weights(group_of):
    return group_of


def stage_moe0_and_maxima(nc, m, gu0, down0):
    PASSES = E0 // G0
    FW = G0 * F0
    SBANKS = REP * 12
    NJ = 2 * TILES0
    with ExitStack() as ctx:
        def sb(name, shape, dt=F32):
            return ctx.enter_context(nc.sbuf_tensor(name, shape, dt))

        def sem(name):
            return ctx.enter_context(nc.semaphore(name))

        ps = m.ps
        wgu = sb("w_gate_up", [P, KT, 2, FW])
        wd = sb("w_down", [P, TILES0, D])
        th = sb("tanh_g", [P, 2, HALF])
        hid = sb("hidden", [P, TILES0, T])
        gs = sb("gate_silu", [P, 2, HALF])
        neg_m = sb("neg_m", [P, NC, NH])
        m3f = sb("m3f", [P, NC, 3, NH])
        m3b = sb("m3b", [P, NC, 3, NH], BF16)
        mT3 = sb("mT3", [3 * NH, T], BF16)
        scratch_m = nc.dram_tensor("scratch_m", [3, NH, T], BF16).ap()
        s_wgu, s_wd = sem("w_gate_up_in"), sem("w_down_in")
        s_gu, s_w, s_th = sem("gate_up_made"), sem("weight_row_made"), sem("tanh_made")
        s_gs, s_hu, s_h = sem("gate_silu_made"), sem("hidden_unscaled"), sem("hidden_made")
        s_dn, s_y = sem("down_made"), sem("down_added")
        s_sc, s_max = sem("scores_made"), sem("scores_maxed")
        s_dve, s_mt, s_mT3 = sem("dve_steps"), sem("m_transposed"), sem("mT3_made")
        s_mst, s_mld = sem("m_stored"), sem("m_stacked")
        block = ctx.enter_context(nc.Block())

        def score_banks(hh):
            for qt in range(NC):
                keys = (qt + 1) * P
                for half in range((keys + HALF - 1) // HALF):
                    yield qt, half, min(HALF, keys - half * HALF)

        @block.sync
        def _(sp):
            with sp.Fori(0, PASSES) as i:
                sp.wait_ge(s_gu, i * NJ + 1)
                sp.dma_start(wgu[:].rearrange("p k g n -> p (k g n)"), gu0[bass.ds(i, 1)].rearrange("i p n -> (i p) n")).then_inc(s_wgu, 16)
                sp.wait_ge(s_dn, i * 4 + 1)
                sp.dma_start(wd[:].rearrange("p t n -> p (t n)"), down0[bass.ds(i, 1)].rearrange("i p n -> (i p) n")).then_inc(s_wd, 16)
            sp.wait_ge(s_mT3, 1)
            sp.dma_start(scratch_m.rearrange("s h t -> (s h) t"), mT3[:]).then_inc(s_mst, 16)
            sp.wait_ge(s_mst, 16)
            sp.dma_start(m.qst[QROWS:QROWS + 3, :, :], scratch_m).then_inc(s_mld, 16)
            sp.wait_ge(s_mld, 16)

        @block.tensor
        def _(pe):
            pe.sem_inc(s_gu, 1)
            pe.sem_inc(s_dn, 1)
            with pe.Fori(0, PASSES) as i:
                def scores(hh, first):
                    pe.wait_ge(s_max, i * SBANKS + first + 1)
                n_bank = 0
                order = [(hh, b) for hh in range(REP) for b in score_banks(hh)]

                def score_bank():
                    nonlocal n_bank
                    hh, (qt, half, cols) = order[n_bank]
                    bank = 6 + n_bank % 2
                    pe.wait_ge(s_max, i * SBANKS + n_bank + 1)
                    diag = half * HALF + cols == (qt + 1) * P
                    mm = pe.matmul(ps[:, bank, 0:cols], m.qst[:, bass.ds(i * REP + hh, 1), qt * P:(qt + 1) * P],
                                   m.kst[:, bass.ds(i, 1), half * HALF:half * HALF + cols],
                                   start=True, stop=not diag)
                    if diag:
                        mm = pe.matmul(ps[:, bank, cols - P:cols], m.future[:], m.identb[:], start=False, stop=True)
                    mm.then_inc(s_sc, 1)
                    n_bank += 1

                pe.wait_ge(s_wgu, i * 16 + 16)
                for j in range(NJ):
                    tile, half = j // 2, j % 2
                    cols = slice(half * HALF, (half + 1) * HALF)
                    gb = 2 * (j % 2)
                    pe.wait_ge(s_hu, i * NJ + j + 1)
                    for which in range(2):
                        for k in range(KT):
                            mm = pe.matmul(ps[:, gb + which, :], wgu[:, k, which, tile * P:(tile + 1) * P],
                                           m.xnT[:, k, cols], start=k == 0, stop=k == KT - 1)
                    mm.then_inc(s_gu, 1)
                    pe.wait_ge(s_h, i * NJ + j + 1)
                    pe.matmul(ps[:, 4, :], m.sel0[0:3 * ESEL, bass.ds(i * FW + tile * P, P)], m.wT3[0:3 * ESEL, cols],
                              start=True, stop=True).then_inc(s_w, 1)
                    for _ in range(5):
                        score_bank()
                pe.wait_ge(s_wd, i * 16 + 16)
                pe.wait_ge(s_h, i * NJ + NJ + 1)
                for c2 in range(NC // 2):
                    pe.wait_ge(s_y, i * 4 + c2 + 1)
                    for c in (2 * c2, 2 * c2 + 1):
                        for t in range(TILES0):
                            mm = pe.matmul(ps[:, 5, (c % 2) * D:(c % 2 + 1) * D], hid[:, t, c * P:(c + 1) * P], wd[:, t, :],
                                           start=t == 0, stop=t == TILES0 - 1)
                    mm.then_inc(s_dn, 1)
                    for _ in range(4 if c2 < 3 else 6):
                        score_bank()
                assert n_bank == SBANKS
            pe.wait_ge(s_dve, 100)
            for c in range(NC):
                mm = pe.transpose(ps[0:3 * NH, c // 4, (c % 4) * P:(c % 4 + 1) * P],
                                  m3f[:, c, :, :].rearrange("p s h -> p (s h)"), m.ident[:])
            mm.then_inc(s_mt, 1)

        @block.scalar
        def _(act):
            with act.Fori(0, PASSES) as i:
                for j in range(NJ):
                    act.wait_ge(s_gu, i * NJ + j + 2)
                    act.wait_ge(s_gs, i * NJ + j + 1)
                    nc.scalar.activation(th[:, j % 2, :], ps[:, 2 * (j % 2), :], ACT.Tanh, scale=0.5).then_inc(s_th, 1)
            act.wait_ge(s_mt, 1)
            nc.scalar.copy(mT3[:], ps[0:3 * NH, 0:2, :].rearrange("p b n -> p (b n)")).then_inc(s_mT3, 1)

        @block.vector
        def _(dve):
            step = Chain(dve, s_dve)
            step.link(dve.memset(m.yacc[:], 0.0))
            dve.sem_inc(s_max, 2)
            dve.sem_inc(s_hu, 2)
            dve.sem_inc(s_gs, 2)
            dve.sem_inc(s_h, 1)
            dve.sem_inc(s_y, 1)
            with dve.Fori(0, PASSES) as i:
                order = [(hh, b) for hh in range(REP) for b in score_banks(hh)]
                n_bank = 0

                def maximum():
                    nonlocal n_bank
                    hh, (qt, half, cols) = order[n_bank]
                    dve.wait_ge(s_sc, i * SBANKS + n_bank + 1)
                    dve.tensor_reduce(m.mpart[:, qt, bass.ds(i * REP + hh, 1), half:half + 1], ps[:, 6 + n_bank % 2, 0:cols],
                                      AX.X, ALU.max).then_inc(s_max, 1)
                    n_bank += 1

                for j in range(NJ):
                    tile, half = j // 2, j % 2
                    cols = slice(half * HALF, (half + 1) * HALF)
                    for _ in range(2):
                        maximum()
                    dve.wait_ge(s_th, i * NJ + j + 1)
                    dve.scalar_tensor_tensor(out=gs[:, j % 2, :], in0=th[:, j % 2, :], scalar=1.0, in1=ps[:, 2 * (j % 2), :],
                                             op0=ALU.add, op1=ALU.mult).then_inc(s_gs, 1)
                    dve.wait_ge(s_gs, i * NJ + j + 3)
                    if j == 0:
                        dve.wait_ge(s_dn, i * 4 + 1)
                    dve.scalar_tensor_tensor(out=hid[:, tile, cols], in0=gs[:, j % 2, :], scalar=0.5,
                                             in1=ps[:, 2 * (j % 2) + 1, :], op0=ALU.mult, op1=ALU.mult).then_inc(s_hu, 1)
                    maximum()
                    dve.wait_ge(s_hu, i * NJ + j + 3)
                    dve.wait_ge(s_w, i * NJ + j + 1)
                    dve.tensor_tensor(hid[:, tile, cols], hid[:, tile, cols], ps[:, 4, :], ALU.mult).then_inc(s_h, 1)
                    for _ in range(2):
                        maximum()
                for c2 in range(NC // 2):
                    dve.wait_ge(s_dn, i * 4 + c2 + 2)
                    dve.tensor_tensor(m.yacc[:, 2 * c2:2 * c2 + 2, :], m.yacc[:, 2 * c2:2 * c2 + 2, :],
                                      ps[:, 5, :].rearrange("p (c d) -> p c d", c=2), ALU.add).then_inc(s_y, 1)
                    for _ in range(4 if c2 < 3 else 6):
                        maximum()
                assert n_bank == SBANKS
            dve.wait_ge(s_max, PASSES * SBANKS + 2)
            step.link(dve.tensor_tensor(neg_m[:, :, :], m.mpart[:, :, :, 0], m.mpart[:, :, :, 1], ALU.max))
            step.link(dve.tensor_scalar(neg_m[:], neg_m[:], -1.0, None, ALU.mult))
            for part in range(3):
                step.link(dve.tensor_copy(m3b[:, :, part, :], neg_m[:]))
                step.link(dve.tensor_copy(m3f[:, :, part, :], m3b[:, :, part, :]))
                if part < 2:
                    step.link(dve.tensor_tensor(neg_m[:], neg_m[:], m3f[:, :, part, :], ALU.subtract))
            dve.sem_inc(s_dve, 100)


def stage_attention(nc, m):
    with ExitStack() as ctx:
        def sb(name, shape, dt=F32):
            return ctx.enter_context(nc.sbuf_tensor(name, shape, dt))

        def sem(name):
            return ctx.enter_context(nc.semaphore(name))

        ps = m.ps
        m.oT = sb("oT", [P, NKV, T])
        vst = sb("v_stage", [P, NC, 32])
        pr = sb("probs", [P, 2, REP, T])
        w_yn = m.xn
        inv = sb("inv_sum", [P, NC, NH])
        yT = m.xnT
        tanh_y = m.oT[:, 0:2, :].rearrange("p g (c d) -> p (g c) d", d=D)
        s_v, s_sc, s_pr, s_pv, s_o = sem("v_staged"), sem("scores_made"), sem("probs_made"), sem("pv_made"), sem("o_copied")
        s_ot, s_inv, s_yn, s_yt, s_yT, s_s, s_dve = (sem("o_transposed"), sem("inv_made"), sem("y_normed"), sem("y_transposed"),
                                              sem("yT_made"), sem("s_made"), sem("dve_steps"))
        block = ctx.enter_context(nc.Block())
        UN = NC * REP

        @block.tensor
        def _(pe):
            pe.sem_inc(s_pv, 2)
            with pe.Fori(0, NKV) as i:
                def pv(kt):
                    pe.wait_ge(s_pr, i * UN + REP * (kt + 1) + 3)
                    if kt == 0:
                        pe.wait_ge(s_v, i + 1)
                        pe.wait_ge(s_o, i + 1)
                    for half in range(2):
                        lo = max(kt * P, half * HALF)
                        hi = (half + 1) * HALF
                        if lo >= hi:
                            continue
                        for h in range(REP):
                            mm = pe.matmul(ps[32 * h:32 * h + 32, 6 + half, lo - half * HALF:HALF], vst[:, kt, :],
                                           pr[:, kt % 2, h, lo - kt * P:hi - kt * P], start=kt == 0, stop=kt == 4 * half + 3)
                    mm.then_inc(s_pv, 1)

                for kt in range(NC):
                    cols = T - kt * P
                    for h in range(REP):
                        n = kt * REP + h
                        b0 = 2 * (n % 3)
                        pe.wait_ge(s_pr, i * UN + n + 1)
                        done = 0
                        while done < cols:
                            w = min(HALF, cols - done)
                            mm = pe.matmul(ps[:, b0 + done // HALF, 0:w], m.kst[:, bass.ds(i, 1), kt * P:(kt + 1) * P],
                                           m.qst[:, bass.ds(i * REP + h, 1), kt * P + done:kt * P + done + w],
                                           start=True, stop=done > 0)
                            if done == 0:
                                mm = pe.matmul(ps[:, b0, 0:P], m.identb[:], m.future[:], start=False, stop=True)
                            done += w
                        mm.then_inc(s_sc, 1)
                    if kt:
                        pv(kt - 1)
                pv(NC - 1)
            for c in range(NC):
                b0 = 2 * (c % 2)
                if c == 0:
                    pe.wait_ge(s_o, NKV + 1)
                if c >= 2:
                    pe.wait_ge(s_yn, c - 1)
                for g in range(NKV):
                    mm = pe.transpose(ps[:, b0 + g // 4, (g % 4) * P:(g % 4 + 1) * P], m.oT[:, g, c * P:(c + 1) * P], m.ident[:])
                mm.then_inc(s_ot, 1)
            pe.wait_ge(s_yn, NC)
            for k in range(KT):
                for c in range(NC):
                    mm = pe.transpose(ps[:, 4 + 2 * k + c // 4, (c % 4) * P:(c % 4 + 1) * P],
                                      w_yn[:, c, k * P:(k + 1) * P], m.ident[:])
            mm.then_inc(s_yt, 1)
            pe.wait_ge(s_yT, 1)
            for c in range(NC):
                for k in range(KT):
                    mm = pe.matmul(ps[:, c // 2, (c % 2) * D:(c % 2 + 1) * D], yT[:, k, c * P:(c + 1) * P], m.w_o[:, k, :],
                                   start=k == 0, stop=k == KT - 1)
            mm.then_inc(s_s, 1)

        @block.scalar
        def _(act):
            act.sem_inc(s_pr, 3)
            with act.Fori(0, NKV) as i:
                for kt in range(NC):
                    cols = T - kt * P
                    act.wait_ge(s_pv, i * NC + kt + 1)
                    for h in range(REP):
                        n = kt * REP + h
                        act.wait_ge(s_sc, i * UN + n + 1)
                        nc.scalar.activation(pr[:, kt % 2, h, 0:cols],
                                             ps[:, 2 * (n % 3):2 * (n % 3) + 2, :].rearrange("p b n -> p (b n)")[:, 0:cols],
                                             ACT.Exp, scale=SCALE).then_inc(s_pr, 1)
            act.wait_ge(s_yt, 1)
            nc.scalar.copy(yT[:].rearrange("p k t -> p (k t)"), ps[:, 4:8, :].rearrange("p b n -> p (b n)")).then_inc(s_yT, 1)
            nc.scalar.activation(tanh_y, m.yacc[:], ACT.Tanh, scale=0.5).then_inc(s_inv, 1)

        @block.vector
        def _(dve):
            step = Chain(dve, s_dve)
            dve.sem_inc(s_o, 1)
            with dve.Fori(0, NKV) as i:
                dve.wait_ge(s_pv, i * NC + 2)
                dve.tensor_copy(vst[:], m.vaug[:, bass.ds(i, 1), :, :].rearrange("p g c d -> p (g c) d")).then_inc(s_v, 1)
                dve.wait_ge(s_pv, (i + 1) * NC + 2)
                dve.tensor_copy(m.oT[:, bass.ds(i, 1), :].rearrange("p g t -> p (g t)"),
                                ps[:, 6:8, :].rearrange("p b n -> p (b n)")).then_inc(s_o, 1)
            for c in range(NC):
                dve.wait_ge(s_ot, c + 1)
                src = ps[:, 2 * (c % 2):2 * (c % 2) + 2, :].rearrange("p b (g d) -> p (b g) d", d=32)
                step.link(dve.reciprocal(inv[:, c, :], src[:, :, HD]))
                dve.tensor_tensor(w_yn[:, c, :].rearrange("p (h d) -> p h d", d=HD), src[:, :, 0:HD],
                                  inv[:, c, :].unsqueeze(2).broadcast_to([P, NH, HD]), ALU.mult).then_inc(s_yn, 1)
            dve.wait_ge(s_inv, 1)
            step.link(dve.scalar_tensor_tensor(out=m.yacc[:], in0=tanh_y, scalar=1.0, in1=m.yacc[:], op0=ALU.add, op1=ALU.mult))
            dve.wait_ge(s_s, 1)
            src = ps[:, 0:4, :].rearrange("p b (c d) -> p (b c) d", d=D)
            step.link(dve.scalar_tensor_tensor(out=m.yacc[:], in0=m.yacc[:], scalar=0.5, in1=src, op0=ALU.mult, op1=ALU.mult))
            step.link(dve.tensor_tensor(m.x[:], m.x[:], m.yacc[:], ALU.add))


def stage_store(nc, m, out):
    with ExitStack() as ctx:
        s_out = ctx.enter_context(nc.semaphore("out_stored"))
        block = ctx.enter_context(nc.Block())

        @block.sync
        def _(sp):
            sp.dma_start(out.rearrange("b (c p) d -> p (b c) d", p=P), m.x[:]).then_inc(s_out, 16)
            sp.wait_ge(s_out, 16)


def stage_l1_inputs(nc, m, router1, w_ba, dt_bias, a_log, norm_w, w_tap):
    with ExitStack() as ctx:
        def sb(name, shape, dt=F32):
            return ctx.enter_context(nc.sbuf_tensor("l1_" + name, shape, dt))

        def sem(name):
            return ctx.enter_context(nc.semaphore(name))

        ps = m.ps
        wr = sb("w_small", [P, KT, E1 + 2 * NV])
        dtb = sb("dt_b", [P, NV])
        alg = sb("a_log_b", [P, NV])
        nw = sb("norm_w_in", [P, 1])
        tap = sb("tap_in", [P, NK + 1, 4, TAPS])
        route = [sb(f"route{i}", [P, NC, E0]) for i in range(5)]
        route_col = [sb(f"route_col{i}", [P, NC]) for i in range(2)]
        w3b = sb("w3b", [P, NC, 3 * ESEL], BF16)
        w3f = sb("w3f", [P, NC, 3 * ESEL])
        za, ea, sa, s2, pol = (sb(f"gate_t{i}", [P, NV, NC]) for i in range(5))
        in_w = sem("small_in")
        s_var, s_rstd, s_tr, s_xnT, s_proj = sem("var"), sem("rstd"), sem("xn_transposed"), sem("xnT_made"), sem("projected")
        s_dve, s_pool, s_zero = sem("dve_steps"), sem("pool_steps"), sem("w3_zeroed")
        s_logit, s_exp, s_w3, s_wt, s_wT3 = (sem("logits_shifted"), sem("exp_made"), sem("w3_split"), sem("w3_transposed"),
                                             sem("wT3_made"))
        s_ab, s_eab, s_g, s_gc, s_eg, s_neg = (sem("ab_shifted"), sem("ab_exped"), sem("g_made"), sem("g_summed"),
                                        sem("decays_made"), sem("decays_negated"))
        block = ctx.enter_context(nc.Block())

        @block.sync
        def _(sp):
            sp.dma_start(wr[:, :, 0:E1], router1.rearrange("(k p) n -> p k n", p=P)).then_inc(in_w, 16)
            sp.dma_start(wr[:, :, E1:], w_ba.rearrange("(k p) n -> p k n", p=P)).then_inc(in_w, 16)
            sp.dma_start(dtb[:], dt_bias.broadcast_to([P, NV])).then_inc(in_w, 16)
            sp.dma_start(alg[:], a_log.broadcast_to([P, NV])).then_inc(in_w, 16)
            sp.dma_start(nw[:], norm_w).then_inc(in_w, 16)
            sp.dma_start(tap[:].rearrange("p a b c -> p (a b c)"), w_tap).then_inc(in_w, 16)

        @block.gpsimd
        def _(pool):
            step = Chain(pool, s_pool)
            nc.gpsimd.memset(w3f[:], 0.0).then_inc(s_zero, 1)
            pool_rsqrt_var(nc, pool, step, m.mv, m.rstd, m.minus_half, s_var, s_rstd)
            step.link(nc.gpsimd.memset(m.sel1[:], 1.0))
            pool_expert_rows(nc, step, m.sel1, F1, E1)

        @block.tensor
        def _(pe):
            pe.wait_ge(s_dve, 2 * NC)
            for k in range(KT):
                for c in range(NC):
                    mm = pe.transpose(ps[:, 2 * k + c // 4, (c % 4) * P:(c % 4 + 1) * P],
                                      m.xn[:, c, k * P:(k + 1) * P], m.ident[:])
                mm.then_inc(s_tr, 1)
            pe.wait_ge(in_w, 96)
            pe.wait_ge(s_xnT, 2)
            for bank, a, n in ((4, 0, E1), (5, E1, 2 * NV)):
                for c in range(NC):
                    for k in range(KT):
                        mm = pe.matmul(ps[:, bank, c * n:(c + 1) * n], m.xnT[:, k, c * P:(c + 1) * P],
                                       wr[:, k, a:a + n], start=k == 0, stop=k == KT - 1)
                mm.then_inc(s_proj, 1)
            pe.wait_ge(s_g, 1)
            gall = m.g[:, 0:NV, :].rearrange("p h c -> p (h c)")
            pe.matmul(ps[:, 6, 0:NV * NC], m.upto[:], gall, start=True, stop=True)
            pe.matmul(ps[:, 6, NV * NC:], m.after[:], gall, start=True, stop=True)
            pe.matmul(ps[:, 7, 0:NV * NC], m.ones[:], gall, start=True, stop=True).then_inc(s_gc, 1)
            pe.wait_ge(s_w3, 1)
            for c in range(NC):
                mm = pe.transpose(ps[0:3 * ESEL, c // 4, (c % 4) * P:(c % 4 + 1) * P], w3f[:, c, :], m.ident[:])
            mm.then_inc(s_wt, 1)

        @block.scalar
        def _(act):
            for k in range(KT):
                act.wait_ge(s_tr, k + 1)
                nc.scalar.copy(m.xnT[:, k, :], ps[:, 2 * k:2 * k + 2, :].rearrange("p b n -> p (b n)")).then_inc(s_xnT, 1)
            act.wait_ge(s_ab, 1)
            nc.scalar.activation(m.beta[:, 0:NV, :], m.beta[:, 0:NV, :], ACT.Exp, scale=-1.0).then_inc(s_eab, 1)
            nc.scalar.activation(ea[:], sa[:], ACT.Exp).then_inc(s_eab, 1)
            nc.scalar.activation(alg[:], alg[:], ACT.Exp).then_inc(s_eab, 1)
            act.wait_ge(s_gc, 1)
            nc.scalar.activation(m.eg[:, 0:2, 0:NV, :].rearrange("p n h c -> p (n h c)"), ps[:, 6, :], ACT.Exp).then_inc(s_eg, 1)
            nc.scalar.activation(m.eg[:, 2, 0:NV, :].rearrange("p h c -> p (h c)"), ps[:, 7, 0:NV * NC], ACT.Exp).then_inc(s_eg, 1)
            act.wait_ge(s_logit, 1)
            nc.scalar.activation(route[1][:, :, 0:E1], route[0][:, :, 0:E1], ACT.Exp).then_inc(s_exp, 1)
            act.wait_ge(s_wt, 1)
            nc.scalar.copy(m.wT3[0:3 * ESEL, :], ps[0:3 * ESEL, 0:2, :].rearrange("p b n -> p (b n)")).then_inc(s_wT3, 1)

        @block.vector
        def _(dve):
            step = Chain(dve, s_dve)
            dve_layer_norm(dve, step, m.x, m.st, m.mv, m.xn, s_var, s_rstd, m.rstd)
            dve.wait_ge(in_w, 96)
            step.link(dve.tensor_scalar(m.norm_w[:], nw[:], 0.5, None, ALU.mult))
            step.link(dve.tensor_scalar(m.taps[:], tap[:], 0.5, None, ALU.mult))
            dve.wait_ge(s_proj, 2)
            ba = ps[:, 5, :].rearrange("p (c n) -> p n c", c=NC)
            full = [P, NV, NC]
            beta, g = m.beta[:, 0:NV, :], m.g[:, 0:NV, :]
            step.link(dve.tensor_copy(beta, ba[:, 0:NV, :]))
            step.link(dve.tensor_tensor(za[:], ba[:, NV:, :], dtb[:].unsqueeze(2).broadcast_to(full), ALU.add))
            step.link(dve.scalar_tensor_tensor(out=sa[:], in0=za[:], scalar=-1.0, in1=za[:], op0=ALU.mult, op1=ALU.min))
            dve.sem_inc(s_ab, 1)
            dve.wait_ge(s_eab, 3)
            step.link(dve.tensor_scalar(beta, beta, 1.0, None, ALU.add))
            step.link(dve.reciprocal(beta, beta))
            step.link(dve.tensor_scalar(sa[:], ea[:], 2.0, None, ALU.add))
            step.link(dve.reciprocal(sa[:], sa[:]))
            step.link(dve.tensor_tensor(sa[:], sa[:], ea[:], ALU.mult))
            step.link(dve.tensor_tensor(s2[:], sa[:], sa[:], ALU.mult))
            step.link(dve.tensor_scalar(pol[:], s2[:], 1.0 / 15, 1.0 / 13, ALU.mult, ALU.add))
            for n in (11, 9, 7, 5, 3, 1):
                step.link(dve.tensor_tensor(pol[:], pol[:], s2[:], ALU.mult))
                step.link(dve.tensor_scalar(pol[:], pol[:], 1.0 / n, None, ALU.add))
            step.link(dve.scalar_tensor_tensor(out=pol[:], in0=pol[:], scalar=2.0, in1=sa[:], op0=ALU.mult, op1=ALU.mult))
            step.link(dve.scalar_tensor_tensor(out=pol[:], in0=za[:], scalar=0.0, in1=pol[:], op0=ALU.max, op1=ALU.add))
            step.link(dve.tensor_tensor(pol[:], pol[:], alg[:].unsqueeze(2).broadcast_to(full), ALU.mult))
            step.link(dve.tensor_scalar(g, pol[:], -1.0, -110.0, ALU.mult, ALU.max))
            dve.tensor_copy(m.g[:, NV:, :], m.g[:, 0:2, :]).then_inc(s_g, 1)
            dve.wait_ge(s_zero, 1)
            dve_route(dve, step, ps[:, 4, 0:NC * E1].rearrange("p (c e) -> p c e", e=E1), E1, TOP1, m.rev,
                      route, route_col, s_logit, s_exp, w3b, w3f)
            dve.sem_inc(s_w3, 1)
            dve.wait_ge(s_eg, 2)
            step.link(dve.tensor_scalar(m.neg_egc[:, :, :], m.eg[:, 0, 0:NV, :], -1.0, None, ALU.mult))


def stage_moe1(nc, m, gu1, down1):
    with ExitStack() as ctx:
        def sb(name, shape, dt=F32):
            return ctx.enter_context(nc.sbuf_tensor("l1_" + name, shape, dt))

        def sem(name):
            return ctx.enter_context(nc.semaphore(name))

        ps = m.ps
        wgu = sb("w_gate_up", [P, KT, 2, P])
        wd = sb("w_down", [P, D])
        th = sb("tanh_g", [P, 2, HALF])
        hid = sb("hidden", [P, T])
        gs = sb("gate_silu", [P, 2, HALF])
        s_wgu, s_wd = sem("w_gate_up_in"), sem("w_down_in")
        s_gu, s_w, s_th = sem("gate_up_made"), sem("weight_row_made"), sem("tanh_made")
        s_gs, s_hu, s_h = sem("gate_silu_made"), sem("hidden_unscaled"), sem("hidden_made")
        s_dn, s_y, s_dve = sem("down_made"), sem("down_added"), sem("dve_steps")
        block = ctx.enter_context(nc.Block())

        @block.sync
        def _(sp):
            with sp.Fori(0, TILES1) as i:
                sp.wait_ge(s_gu, i * 2 + 1)
                sp.dma_start(wgu[:].rearrange("p k g n -> p (k g n)"), gu1[bass.ds(i, 1)].rearrange("i p n -> (i p) n")).then_inc(s_wgu, 16)
                sp.wait_ge(s_dn, i * 4 + 1)
                sp.dma_start(wd[:], down1[bass.ds(i, 1)].rearrange("i p n -> (i p) n")).then_inc(s_wd, 16)

        @block.tensor
        def _(pe):
            pe.sem_inc(s_gu, 1)
            pe.sem_inc(s_dn, 1)
            with pe.Fori(0, TILES1) as i:
                pe.wait_ge(s_wgu, i * 16 + 16)
                for half in range(2):
                    cols = slice(half * HALF, (half + 1) * HALF)
                    pe.wait_ge(s_hu, i * 2 + half + 1)
                    for which in range(2):
                        for k in range(KT):
                            mm = pe.matmul(ps[:, 2 * half + which, :], wgu[:, k, which, :], m.xnT[:, k, cols],
                                           start=k == 0, stop=k == KT - 1)
                    mm.then_inc(s_gu, 1)
                    pe.wait_ge(s_h, i * 2 + half + 1)
                    pe.matmul(ps[:, 4, :], m.sel1[0:3 * ESEL, bass.ds(i * P, P)], m.wT3[0:3 * ESEL, cols],
                              start=True, stop=True).then_inc(s_w, 1)
                pe.wait_ge(s_wd, i * 16 + 16)
                pe.wait_ge(s_h, i * 2 + 3)
                for c2 in range(NC // 2):
                    pe.wait_ge(s_y, i * 4 + c2 + 1)
                    for c in (2 * c2, 2 * c2 + 1):
                        mm = pe.matmul(ps[:, 5 + c2 % 2, (c % 2) * D:(c % 2 + 1) * D], hid[:, c * P:(c + 1) * P], wd[:],
                                       start=True, stop=True)
                    mm.then_inc(s_dn, 1)

        @block.scalar
        def _(act):
            with act.Fori(0, TILES1) as i:
                for half in range(2):
                    act.wait_ge(s_gu, i * 2 + half + 2)
                    act.wait_ge(s_gs, i * 2 + half + 1)
                    nc.scalar.activation(th[:, half, :], ps[:, 2 * half, :], ACT.Tanh, scale=0.5).then_inc(s_th, 1)

        @block.vector
        def _(dve):
            step = Chain(dve, s_dve)
            step.link(dve.memset(m.yacc[:], 0.0))
            dve.sem_inc(s_hu, 2)
            dve.sem_inc(s_gs, 2)
            dve.sem_inc(s_h, 1)
            dve.sem_inc(s_y, 2)
            with dve.Fori(0, TILES1) as i:
                for half in range(2):
                    cols = slice(half * HALF, (half + 1) * HALF)
                    dve.wait_ge(s_th, i * 2 + half + 1)
                    dve.scalar_tensor_tensor(out=gs[:, half, :], in0=th[:, half, :], scalar=1.0, in1=ps[:, 2 * half, :],
                                             op0=ALU.add, op1=ALU.mult).then_inc(s_gs, 1)
                    dve.wait_ge(s_gs, i * 2 + half + 3)
                    dve.wait_ge(s_dn, i * 4 + 1)
                    dve.scalar_tensor_tensor(out=hid[:, cols], in0=gs[:, half, :], scalar=0.5, in1=ps[:, 2 * half + 1, :],
                                             op0=ALU.mult, op1=ALU.mult).then_inc(s_hu, 1)
                    dve.wait_ge(s_hu, i * 2 + half + 3)
                    dve.wait_ge(s_w, i * 2 + half + 1)
                    dve.tensor_tensor(hid[:, cols], hid[:, cols], ps[:, 4, :], ALU.mult).then_inc(s_h, 1)
                for c2 in range(NC // 2):
                    dve.wait_ge(s_dn, i * 4 + c2 + 2)
                    dve.tensor_tensor(m.yacc[:, 2 * c2:2 * c2 + 2, :], m.yacc[:, 2 * c2:2 * c2 + 2, :],
                                      ps[:, 5 + c2 % 2, :].rearrange("p (c d) -> p c d", c=2), ALU.add).then_inc(s_y, 1)


def inverse_steps():
    steps = [("X", 0, 1)]
    for lv in range(1, LEVELS):
        if lv > 1:
            steps += [("Y", 1, lv - 1), ("YT", 1, lv - 1)]
        if lv < LEVELS - 1:
            steps.append(("Y", 0, lv))
        steps += [("YT", 0, lv), ("X", 1, lv)]
        if lv < LEVELS - 1:
            steps.append(("X", 0, lv + 1))
    steps.append(("YT", 1, LEVELS - 1))
    return steps


def stage_delta(nc, m, w_conv, w_z, w_out, out):
    with ExitStack() as ctx:
        def sb(name, shape, dt=F32):
            return ctx.enter_context(nc.sbuf_tensor(name, shape, dt))

        def sem(name):
            return ctx.enter_context(nc.semaphore(name))

        ps = m.ps
        wc = sb("w_conv_st", [P, KT, 4 * P])
        wz = sb("w_z_st", [P, KT, 2 * P])
        wo = sb("w_out_st", [P, 2, D])
        tap = sb("tap_st", [P, 4, TAPS])
        raw = sb("raw", [P, 4, TAPS - 1 + T])
        cv = sb("conv", [P, 4, T])
        thc = sb("tanh_conv", [P, T])
        kq = sb("kq", [P, NC, 2, P])
        ss = sb("sumsq", [P, 2, NC])
        rs = sb("rsqrt", [P, 2, NC])
        irk = sb("norm_k", [P, NC])
        NAMES = {n: i for i, n in enumerate(("a1", "a1_after", "egc_rq", "neg_egc", "etot"))}
        scal = sb("unit_scalars", [P, len(NAMES), 2, NC])
        knat = sb("k_nat", [P, NC, P])
        vnat = sb("v_nat", [P, 2, NC, P])
        gm_q = sb("gmask_Q", [P, 2, NC, P])
        e_p = sb("decay_P", [P, 2, NC, P])
        att = sb("att", [P, 2, NC, P])
        sq = att[:].rearrange("p e c i -> p e (c i)")
        u = sb("U", [P, 2, NC, P])
        xs = sb("X", [P, LEVELS - 1, NC, P])
        st = sb("S", [P, 2, P])
        wsb = sb("W", [P, 2, 2, P])
        qs = sb("QS", [P, 2, P])
        tz = sb("tanh_z", [P, 2 * P])
        zs = sb("silu_z", [P, NC, 2 * P])
        o = sb("o", [P, NC, 2, P])
        og = sb("o_gated", [P, NC, 2, P])
        osq = sb("o_squares", [P, P])
        var = sb("o_var", [P, NC, 2])
        ro = sb("o_rsqrt", [P, NC, 2])
        oT = m.xn[:].rearrange("p c d -> p (c d)").rearrange("p (e t) -> p e t", e=2)
        y = sb("y_delta", [P, NC, D])

        s_wc, s_wz, s_wo = sem("w_conv_in"), sem("w_z_in"), sem("w_out_in")
        s_pj, s_raw, s_conv, s_tc, s_cvd = (sem("projected"), sem("raw_copied"), sem("convolved"), sem("conv_tanh"),
                                            sem("conv_done"))
        s_tap, s_dconv = sem("taps_staged"), sem("tap_added")
        s_sq, s_ss, s_sse, s_sc = sem("squared"), sem("sumsq_made"), sem("sumsq_eps"), sem("scalars_made")
        s_gm, s_kq, s_d, s_e, s_kk, s_u = (sem("gmask_made"), sem("kq_copied"), sem("D_made"), sem("E_made"), sem("kk_made"),
                                           sem("U_made"))
        s_p, s_kt, s_kn, s_vn, s_qt, s_q = (sem("P_begun"), sem("kv_transposed"), sem("k_nat_made"), sem("v_nat_made"),
                                            sem("Q_transposed"), sem("Q_begun"))
        s_iv, s_tk = sem("inverse_made"), sem("inverse_taken")
        s_ot, s_ote, s_op, s_ya = sem("o_transposed"), sem("oT_made"), sem("out_made"), sem("y_added")
        s_ks, s_qsm, s_r, s_w, s_wa, s_ws = (sem("KS_made"), sem("QS_made"), sem("R_made"), sem("W_made"), sem("Wa_made"),
                                             sem("Ws_made"))
        s_su, s_S, s_aw, s_qe, s_o = sem("S_update"), sem("S_made"), sem("AW_made"), sem("QS_scaled"), sem("O_made")
        s_zp, s_tz, s_zs, s_oz, s_var, s_rr, s_og = (sem("z_made"), sem("z_tanh"), sem("z_silu"), sem("oz_made"),
                                                     sem("o_var_made"), sem("o_rsqrt_made"), sem("og_made"))
        s_dve, s_pool, s_init, s_passed = sem("dve_steps"), sem("pool_steps"), sem("buffers_zeroed"), sem("pool_wait_passed")
        s_out = sem("out_stored")
        steps = inverse_steps()
        NI = len(steps)
        index = {s: n for n, s in enumerate(steps)}
        block = ctx.enter_context(nc.Block())

        def cols(ap, lv, half):
            s = 1 << lv
            return ap.rearrange("p (b t s) -> p b t s", t=2, s=s)[:, :, half, :]

        def sc(name, e, c):
            return scal[:, NAMES[name], e, c:c + 1]

        @block.sync
        def _(sp):
            sp.dma_start(wc[:].rearrange("p k n -> p (k n)"), w_conv[0]).then_inc(s_wc, 16)
            sp.dma_start(wo[:].rearrange("p e n -> p (e n)"), w_out[0]).then_inc(s_wo, 16)
            with sp.Fori(0, NK) as i:
                sp.wait_ge(s_pj, i * 8 + 8)
                sp.dma_start(wc[:].rearrange("p k n -> p (k n)"), w_conv[bass.ds(i + 1, 1)].rearrange("i p n -> (i p) n")).then_inc(s_wc, 16)
                sp.wait_ge(s_zp, i * NC + 1)
                sp.dma_start(wz[:].rearrange("p k n -> p (k n)"), w_z[bass.ds(i, 1)].rearrange("i p n -> (i p) n")).then_inc(s_wz, 16)
                sp.wait_ge(s_op, i * 4 + 4)
                sp.dma_start(wo[:].rearrange("p e n -> p (e n)"), w_out[bass.ds(i, 1)].rearrange("i p n -> (i p) n")).then_inc(s_wo, 16)
            sp.wait_ge(s_wc, 16 * (NK + 1))
            sp.wait_ge(s_wz, 16 * NK)

        @block.tensor
        def _(pe):
            pe.sem_inc(s_zp, 1)

            def project(r, n):
                if n == 0:
                    pe.wait_ge(s_wc, r * 16 + 16)
                if isinstance(r, int) and n < 2:
                    pass
                else:
                    pe.wait_ge(s_raw, r * 8 + n - 1)
                for k in range(KT):
                    mm = pe.matmul(ps[:, 4 + n % 2, :], wc[:, k, (n // 2) * P:(n // 2 + 1) * P],
                                   m.xnT[:, k, (n % 2) * HALF:(n % 2 + 1) * HALF], start=k == 0, stop=k == KT - 1)
                mm.then_inc(s_pj, 1)

            def turn_outputs(i, n):
                e, half = n // 2, n % 2
                if n == 0:
                    pe.wait_ge(s_og, i + 1)
                if n >= 2:
                    pe.wait_ge(s_ote, i * 4 + n - 1)
                for c in range(4):
                    mm = pe.transpose(ps[:, 6 + n % 2, c * P:(c + 1) * P], og[:, 4 * half + c, e, :], m.ident[:])
                mm.then_inc(s_ot, 1)

            def project_out(i, n):
                if n == 0:
                    pe.wait_ge(s_wo, i * 16 + 16)
                    pe.wait_ge(s_ote, i * 4 + 4)
                if n >= 2:
                    pe.wait_ge(s_ya, i * 4 + n)
                for c in (2 * n, 2 * n + 1):
                    for e in range(2):
                        mm = pe.matmul(ps[:, 6 + n % 2, (c % 2) * D:(c % 2 + 1) * D], oT[:, e, c * P:(c + 1) * P], wo[:, e, :],
                                       start=e == 0, stop=e == 1)
                mm.then_inc(s_op, 1)

            for n in range(8):
                project(0, n)
            with pe.Fori(0, NK) as i:
                pe.wait_ge(s_gm, i + 1)
                pe.wait_ge(s_o, i * NC + 1)
                pe.wait_ge(s_zs, i * NC + 1)
                pe.wait_ge(s_ya, i * 4 + 1)
                for b in range(4):
                    pe.matmul(ps[:, b, :], m.after[:], gm_q[:, b // 2, 4 * (b % 2):4 * (b % 2) + 4, :].rearrange("p c i -> p (c i)"),
                              start=True, stop=False)
                    mm = pe.matmul(ps[:, b, :], m.identb[:], m.future[:].unsqueeze(1).broadcast_to([P, 4, P]),
                                   start=False, stop=True)
                    mm.then_inc(s_d, 1)
                pe.wait_ge(s_sq, i * 2 + 2)
                for n in range(2):
                    for c in range(NC):
                        mm = pe.matmul(ps[:, 7, n * NC + c:n * NC + c + 1], sq[:, n, c * P:(c + 1) * P], m.ones[:, 0:1],
                                       start=True, stop=True)
                mm.then_inc(s_ss, 1)
                pe.wait_ge(s_kq, i + 1)
                pe.wait_ge(s_raw, i * 8 + 8)
                for b in range(4):
                    if b == 3:
                        pe.wait_ge(s_sse, i + 1)
                    for c in (2 * b, 2 * b + 1):
                        mm = pe.matmul(ps[:, 4 + b, (c % 2) * 256:(c % 2 + 1) * 256], kq[:, c, 0, :],
                                       kq[:, c, :, :].rearrange("p a i -> p (a i)"), start=True, stop=True)
                    mm.then_inc(s_kk, 1)
                pe.wait_ge(s_cvd, i * 4 + 4)
                pe.wait_ge(s_e, i * 4 + 2)
                for n, b0 in ((1, 0), (2, 2), (3, 4)):
                    if n == 2:
                        pe.wait_ge(s_e, i * 4 + 4)
                    if n == 3:
                        pe.wait_ge(s_u, i * 4 + 2)
                    for c in range(NC):
                        mm = pe.transpose(ps[:, b0 + c // 4, (c % 4) * P:(c % 4 + 1) * P], cv[:, n, c * P:(c + 1) * P], m.ident[:])
                    mm.then_inc(s_kt, 1)
                for e in range(2):
                    pe.wait_ge(s_p, i * 2 + e + 1)
                    if e == 0:
                        pe.wait_ge(s_u, i * 4 + 4)
                    else:
                        pe.wait_ge(s_kn, i + 1)
                    for c in range(NC):
                        b0 = (6, 0)[e]
                        mm = pe.transpose(ps[:, b0 + c // 4, (c % 4) * P:(c % 4 + 1) * P], e_p[:, e, c, :], m.ident[:])
                    mm.then_inc(s_qt, 1)
                pe.wait_ge(s_vn, i * 2 + 2)
                pe.wait_ge(s_q, i * 2 + 2)
                between = {5 + 2 * n: (turn_outputs, n) for n in range(4)} | {14 + 4 * n: (project_out, n) for n in range(4)}
                for n, (kind, e, lv) in enumerate(steps):
                    need = []
                    if kind == "X" and lv > 1:
                        need = [("Y", e, lv - 1)]
                    if kind != "X":
                        need = [("X", e, lv)] + ([("YT", e, lv - 1)] if lv > 1 else [])
                    if need:
                        pe.wait_ge(s_tk, i * NI + max(index[s] for s in need) + 1)
                    bank = {"X": 2, "Y": 4, "YT": 0}[kind] + e
                    for c in range(NC):
                        dst = ps[:, bank, c * 64:(c + 1) * 64].rearrange("p (b s) -> p b s", s=1 << lv)
                        if kind == "X":
                            mm = pe.matmul(dst, u[:, e, c, :], cols(gm_q[:, e, c, :], lv, 0), start=True, stop=True)
                        elif kind == "Y":
                            mm = pe.matmul(dst, e_p[:, e, c, :], cols(xs[:, lv - 1, c, :], lv, 0), start=True, stop=True)
                        else:
                            mm = pe.matmul(dst, xs[:, lv - 1, c, :], cols(e_p[:, e, c, :], lv, 1), start=True, stop=True)
                    mm.then_inc(s_iv, 1)
                    if n in between:
                        what, k = between[n]
                        what(i, k)
                pe.wait_ge(s_tk, i * NI + NI)
                for c in range(NC):
                    if c:
                        pe.wait_ge(s_S, i * 7 + c)
                        pe.wait_ge(s_qe, i * 7 + c - 1) if c > 1 else None
                        state = st[:].rearrange("p e n -> p (e n)")
                        pe.matmul(ps[:, 0, 0:256], kq[:, c, 0, :], state, start=True, stop=True).then_inc(s_ks, 1)
                        pe.matmul(ps[:, 6, 0:256], kq[:, c, 1, :], state, start=True, stop=True).then_inc(s_qsm, 1)
                    project(i + 1, c)
                    if c:
                        pe.wait_ge(s_r, i * 7 + c)
                        pe.wait_ge(s_wa, i * NC + c)
                    for e in range(2):
                        mm = pe.matmul(ps[:, 1, e * P:(e + 1) * P], e_p[:, e, c, :], vnat[:, e, c, :], start=True, stop=True)
                    mm.then_inc(s_w, 1)
                    if c == 0:
                        pe.wait_ge(s_wz, i * 16 + 16)
                    pe.wait_ge(s_zs, i * NC + c + 1)
                    for k in range(KT):
                        mm = pe.matmul(ps[:, 3, 0:256], m.xnT[:, k, c * P:(c + 1) * P], wz[:, k, :], start=k == 0, stop=k == KT - 1)
                    mm.then_inc(s_zp, 1)
                    if c:
                        pe.wait_ge(s_o, i * NC + c + 1)
                    if c < NC - 1:
                        pe.wait_ge(s_ws, i * 7 + c + 1)
                        pe.matmul(ps[:, 2, 0:256], knat[:, c, :], wsb[:, 1, :, :].rearrange("p e n -> p (e n)"),
                                  start=True, stop=True).then_inc(s_su, 1)
                    pe.wait_ge(s_wa, i * NC + c + 1)
                    for e in range(2):
                        mm = pe.matmul(ps[:, 7, e * P:(e + 1) * P], att[:, e, c, :], wsb[:, 0, e, :], start=True, stop=True)
                    mm.then_inc(s_aw, 1)
            pe.wait_ge(s_ya, NK * 4 + 1)
            for n in range(4):
                turn_outputs(NK, n)
            for n in range(4):
                project_out(NK, n)

        @block.scalar
        def _(act):
            def copy_raw(r, n):
                pj = r * 8 + n + 1
                act.wait_ge(s_pj, pj)
                if isinstance(r, int):
                    if n == 0:
                        act.wait_ge(s_init, 2)
                else:
                    act.wait_ge(s_conv, r * 4 + (n // 2) - 3)
                at = TAPS - 1 + (n % 2) * HALF
                nc.scalar.copy(raw[:, n // 2, at:at + HALF], ps[:, 4 + n % 2, :]).then_inc(s_raw, 1)

            def tanh_conv(r, t):
                act.wait_ge(s_conv, r * 4 + t + 1)
                if not (isinstance(r, int) and t == 0):
                    act.wait_ge(s_cvd, r * 4 + t)
                nc.scalar.activation(thc[:], cv[:, t, :], ACT.Tanh).then_inc(s_tc, 1)

            def variance(i, c):
                act.wait_ge(s_o, i * NC + c + 2)
                for e in range(2):
                    op = nc.scalar.activation(osq[:], o[:, c, e, :], ACT.Square, accum_out=var[:, c, e:e + 1])
                    op.then_inc(s_var, 1)
                    act.wait_ge(s_var, i * 16 + 2 * c + e + 1)

            for n in range(8):
                copy_raw(0, n)
            for t in range(4):
                tanh_conv(0, t)

            def turn_out(i, n):
                act.wait_ge(s_ot, i * 4 + n + 1)
                e, half = n // 2, n % 2
                nc.scalar.activation(oT[:, e, half * HALF:(half + 1) * HALF], ps[:, 6 + n % 2, :], ACT.Copy,
                                     scale=m.norm_w[:, 0:1]).then_inc(s_ote, 1)

            with act.Fori(0, NK) as i:
                act.wait_ge(s_cvd, i * 4 + 2)
                act.wait_ge(s_o, i * NC + 1)
                for n in range(2):
                    nc.scalar.activation(sq[:, n, :], cv[:, n, :], ACT.Square).then_inc(s_sq, 1)
                for b in range(4):
                    act.wait_ge(s_d, i * 4 + b + 1)
                    nc.scalar.activation(e_p[:, b // 2, 4 * (b % 2):4 * (b % 2) + 4, :].rearrange("p c i -> p (c i)"),
                                         ps[:, b, :], ACT.Exp).then_inc(s_e, 1)
                act.wait_ge(s_kt, i * 3 + 1)
                nc.scalar.copy(knat[:].rearrange("p c i -> p (c i)"), ps[:, 0:2, :].rearrange("p b n -> p (b n)")).then_inc(s_kn, 1)
                for e in range(2):
                    act.wait_ge(s_qt, i * 2 + e + 1)
                    b0 = (6, 0)[e]
                    nc.scalar.copy(gm_q[:, e, :, :].rearrange("p c i -> p (c i)"),
                                   ps[:, b0:b0 + 2, :].rearrange("p b n -> p (b n)")).then_inc(s_q, 1)
                for n in range(4):
                    turn_out(i, n)
                for c in range(NC):
                    if c:
                        act.wait_ge(s_qsm, i * 7 + c)
                        act.wait_ge(s_o, i * NC + c + 1)
                        for e in range(2):
                            op = nc.scalar.activation(qs[:, e, :], ps[:, 6, e * P:(e + 1) * P], ACT.Copy,
                                                      scale=sc("egc_rq", e, c))
                        op.then_inc(s_qe, 1)
                    act.wait_ge(s_w, i * NC + c + 1)
                    if c < NC - 1:
                        act.wait_ge(s_ws, i * 7 + c + 1)
                    for e in range(2):
                        op = nc.scalar.activation(wsb[:, 0, e, :], ps[:, 1, e * P:(e + 1) * P], ACT.Copy, scale=sc("a1", e, c))
                    op.then_inc(s_wa, 1)
                    copy_raw(i + 1, c)
                    act.wait_ge(s_zp, i * NC + c + 2)
                    act.wait_ge(s_zs, i * NC + c + 1)
                    nc.scalar.activation(tz[:], ps[:, 3, 0:256], ACT.Tanh, scale=0.5).then_inc(s_tz, 1)
                    if c:
                        variance(i, c - 1)
                    if c >= 3 and c % 2:
                        tanh_conv(i + 1, (c - 3) // 2)
                variance(i, NC - 1)
                tanh_conv(i + 1, 3)
            for n in range(4):
                turn_out(NK, n)
            nc.scalar.activation(zs[:], m.yacc[:], ACT.Tanh, scale=0.5).then_inc(s_tz, 1)

        @block.gpsimd
        def _(pool):
            step = Chain(pool, s_pool)
            g = nc.gpsimd

            def gmask(r):
                gsrc = m.g[:, 0:2, :] if isinstance(r, int) else m.g[:, bass.ds(2 * r, 2), :]
                g.tensor_tensor(gm_q[:], m.upto[:].unsqueeze(1).unsqueeze(1).broadcast_to([P, 2, NC, P]),
                                gsrc.unsqueeze(3).broadcast_to([P, 2, NC, P]), ALU.mult).then_inc(s_gm, 1)

            g.tensor_copy(tap[:], m.taps[:, 0, :, :]).then_inc(s_tap, 1)
            g.memset(raw[:, :, 0:TAPS - 1], 0.0).then_inc(s_init, 1)
            g.memset(xs[:], 0.0).then_inc(s_init, 1)
            gmask(0)
            with pool.Fori(0, NK) as i:
                KP = 6
                step = Chain(pool, s_pool, i * KP)

                def passed():
                    pool.sem_inc(s_passed, 1)

                pool.wait_ge(s_cvd, i * 4 + 2)
                pool.wait_ge(s_o, i * NC + 1)
                passed()
                step(g.tensor_copy(kq[:, :, 1, :], cv[:, 0, :].rearrange("p (c i) -> p c i", i=P)))
                g.tensor_copy(kq[:, :, 0, :], cv[:, 1, :].rearrange("p (c i) -> p c i", i=P)).then_inc(s_kq, 1)
                pool.wait_ge(s_sse, i + 1)
                step(g.tensor_tensor(rs[:], ss[:], m.minus_half[:, 0:1].unsqueeze(2).broadcast_to([P, 2, NC]), ALU.pow))
                step(g.tensor_tensor(irk[:], ss[:, 1, :], m.plus_half[:, 0:1].broadcast_to([P, NC]), ALU.pow))
                step.wait()
                passed()
                step(g.tensor_scalar(rs[:, 0, :], rs[:, 0, :], float(DK) ** -0.5, None, ALU.mult))
                step.link(g.tensor_tensor(rs[:, 1, :], rs[:, 1, :], rs[:, 1, :], ALU.mult))
                both = [P, 2, NC]
                rk2 = rs[:, 1, :].unsqueeze(1).broadcast_to(both)
                rq = rs[:, 0, :].unsqueeze(1).broadcast_to(both)
                heads = bass.ds(2 * i, 2)
                step.link(g.tensor_tensor(scal[:, NAMES["a1"]], m.beta[:, heads, :], rk2, ALU.mult))
                g.tensor_tensor(scal[:, NAMES["a1_after"]], m.eg[:, 1, heads, :], scal[:, NAMES["a1"]], ALU.mult).then_inc(s_sc, 1)
                g.tensor_tensor(scal[:, NAMES["egc_rq"]], m.eg[:, 0, heads, :], rq, ALU.mult).then_inc(s_sc, 1)
                passed()
                g.tensor_copy(scal[:, NAMES["neg_egc"]], m.neg_egc[:, heads, :]).then_inc(s_sc, 1)
                g.tensor_copy(scal[:, NAMES["etot"]], m.eg[:, 2, heads, :]).then_inc(s_sc, 1)
                assert step.n == KP
                pool.wait_ge(s_u, i * 4 + 4)
                for e in range(2):
                    g.tensor_tensor(e_p[:, e], u[:, e], m.pair_mask[:].rearrange("p b t -> p (b t)").unsqueeze(1).broadcast_to([P, NC, P]),
                                    ALU.mult).then_inc(s_init, 1)
                    pool.wait_ge(s_init, i * 2 + e + 3)
                    g.tensor_tensor(e_p[:, e], e_p[:, e], m.ident[:].unsqueeze(1).broadcast_to([P, NC, P]), ALU.add).then_inc(s_p, 1)
                pool.wait_ge(s_iv, i * NI + NI)
                pool.wait_ge(s_tk, i * NI + NI)
                gmask(i + 1)
                pool.wait_ge(s_cvd, i * 4 + 4)
                passed()
                g.tensor_copy(tap[:], m.taps[:, bass.ds(i + 1, 1), :, :].rearrange("p a b c -> p (a b) c")).then_inc(s_tap, 1)
                pool.wait_ge(s_ot, i * 4 + 4)
                for c in range(NC):
                    pool.wait_ge(s_o, i * NC + c + 2)
                    pool.wait_ge(s_zs, i * NC + c + 2)
                    g.tensor_tensor(og[:, c].rearrange("p e n -> p (e n)"), o[:, c].rearrange("p e n -> p (e n)"), zs[:, c, :],
                                    ALU.mult).then_inc(s_oz, 1)
                pool.wait_ge(s_var, i * 16 + 16)
                passed()
                g.tensor_scalar(ro[:], var[:], 1.0 / DK, 1e-6, ALU.mult, ALU.add).then_inc(s_rr, 1)
                pool.wait_ge(s_rr, i * 2 + 1)
                g.tensor_tensor(ro[:], ro[:], m.minus_half[:, 0:1].unsqueeze(2).broadcast_to([P, NC, 2]), ALU.pow).then_inc(s_rr, 1)

        @block.vector
        def _(dve):
            step = Chain(dve, s_dve)

            def conv_op(r, t, k):
                if k == 0:
                    dve.wait_ge(s_raw, r * 8 + 2 * t + 2)
                    dve.wait_ge(s_tap, r + 1)
                at = TAPS - 1 - k
                if k == 0:
                    op = dve.tensor_scalar(cv[:, t, :], raw[:, t, at:at + T], tap[:, t, TAPS - 1:TAPS], None, ALU.mult)
                elif k < TAPS:
                    op = dve.scalar_tensor_tensor(out=cv[:, t, :], in0=raw[:, t, at:at + T], scalar=tap[:, t, at:at + 1],
                                                  in1=cv[:, t, :], op0=ALU.mult, op1=ALU.add)
                if k < TAPS - 1:
                    op.then_inc(s_dconv, 1)
                    dve.wait_ge(s_dconv, r * 12 + t * 3 + k + 1)
                elif k == TAPS - 1:
                    op.then_inc(s_conv, 1)
                else:
                    dve.wait_ge(s_tc, r * 4 + t + 1)
                    dve.scalar_tensor_tensor(out=cv[:, t, :], in0=thc[:], scalar=1.0, in1=cv[:, t, :],
                                             op0=ALU.add, op1=ALU.mult).then_inc(s_cvd, 1)

            def add_out(i, n):
                dve.wait_ge(s_op, i * 4 + n + 1)
                dve.tensor_tensor(y[:, 2 * n:2 * n + 2, :], y[:, 2 * n:2 * n + 2, :],
                                  ps[:, 6 + n % 2, :].rearrange("p (c d) -> p c d", c=2), ALU.add).then_inc(s_ya, 1)

            step.link(dve.memset(y[:], 0.0))
            dve.sem_inc(s_o, 1)
            dve.sem_inc(s_zs, 1)
            dve.sem_inc(s_ya, 1)
            dve.memset(og[:], 0.0).then_inc(s_og, 1)
            dve.wait_ge(s_init, 1)
            for t in range(4):
                for k in range(TAPS + 1):
                    conv_op(0, t, k)
            with dve.Fori(0, NK) as i:
                dve.wait_ge(s_ss, i + 1)
                dve.tensor_scalar(ss[:].rearrange("p n c -> p (n c)"), ps[:, 7, 0:2 * NC], 1e-6, None, ALU.add).then_inc(s_sse, 1)
                dve.wait_ge(s_sc, i * 4 + 4)
                dve.wait_ge(s_e, i * 4 + 4)
                for b in range(4):
                    dve.wait_ge(s_kk, i * 4 + b + 1)
                    kk = ps[:, 4 + b, :].rearrange("p (c a n) -> p c a n", c=2, a=2)
                    for e in range(2):
                        dve.tensor_tensor(att[:, e, 2 * b:2 * b + 2, :], kk[:, :, 1, :], e_p[:, e, 2 * b:2 * b + 2, :], ALU.mult)
                        for c in (2 * b, 2 * b + 1):
                            op = dve.scalar_tensor_tensor(out=u[:, e, c, :], in0=kk[:, c % 2, 0, :], scalar=sc("a1", e, c),
                                                          in1=e_p[:, e, c, :], op0=ALU.mult, op1=ALU.mult)
                    op.then_inc(s_u, 1)
                for e in range(2):
                    dve.wait_ge(s_kt, i * 3 + e + 2)
                    dve.tensor_tensor(vnat[:, e], ps[:, 2 + 2 * e:4 + 2 * e, :].rearrange("p b (c n) -> p (b c) n", n=P),
                                      irk[:].unsqueeze(2).broadcast_to([P, NC, P]), ALU.mult).then_inc(s_vn, 1)
                add_at = {18 + 4 * n: n for n in range(4)}
                for n, (kind, e, lv) in enumerate(steps):
                    dve.wait_ge(s_iv, i * NI + n + 1)
                    bank = {"X": 2, "Y": 4, "YT": 0}[kind] + e
                    s = 1 << lv
                    src = ps[:, bank, :].rearrange("p (c b s) -> p c b s", c=NC, s=s)
                    if kind == "X":
                        dst = xs[:, lv - 1, :, :].rearrange("p c (b t s) -> p c b t s", t=2, s=s)[:, :, :, 0, :]
                        mask = m.lmask[:, lv, :].rearrange("p (b s) -> p b s", s=s).unsqueeze(1).broadcast_to([P, NC, 64 // s, s])
                        op = dve.tensor_tensor(dst, src, mask, ALU.mult)
                    else:
                        buf, half = (gm_q, 0) if kind == "Y" else (e_p, 1)
                        dst = buf[:, e, :, :].rearrange("p c (b t s) -> p c b t s", t=2, s=s)[:, :, :, half, :]
                        op = dve.tensor_tensor(dst, dst, src, ALU.subtract)
                    op.then_inc(s_tk, 1)
                    if n in add_at:
                        add_out(i, add_at[n])
                dve.wait_ge(s_kq, i + 1)
                dve.wait_ge(s_kt, i * 3 + 3)
                for c in range(NC):
                    conv = []
                    if c >= 2:
                        t = (c - 2) // 2
                        conv = [(t, 0), (t, 1)] if c % 2 == 0 else [(t, 2), (t, 3), (t, 4)]
                    conv = list(conv)
                    if c:
                        dve.wait_ge(s_ks, i * 7 + c)
                        for e in range(2):
                            op = dve.scalar_tensor_tensor(out=vnat[:, e, c, :], in0=ps[:, 0, e * P:(e + 1) * P],
                                                          scalar=sc("neg_egc", e, c), in1=vnat[:, e, c, :],
                                                          op0=ALU.mult, op1=ALU.add)
                        op.then_inc(s_r, 1)
                    if conv:
                        conv_op(i + 1, *conv.pop(0))
                    dve.wait_ge(s_w, i * NC + c + 1)
                    if c < NC - 1:
                        for e in range(2):
                            op = dve.tensor_scalar(wsb[:, 1, e, :], ps[:, 1, e * P:(e + 1) * P], sc("a1_after", e, c), None, ALU.mult)
                        op.then_inc(s_ws, 1)
                    if conv:
                        conv_op(i + 1, *conv.pop(0))
                    if c < NC - 1:
                        dve.wait_ge(s_su, i * 7 + c + 1)
                        if c == 0:
                            op = dve.tensor_copy(st[:], ps[:, 2, 0:256].rearrange("p (e n) -> p e n", e=2))
                        else:
                            for e in range(2):
                                op = dve.scalar_tensor_tensor(out=st[:, e, :], in0=st[:, e, :], scalar=sc("etot", e, c),
                                                              in1=ps[:, 2, e * P:(e + 1) * P], op0=ALU.mult, op1=ALU.add)
                        op.then_inc(s_S, 1)
                    dve.wait_ge(s_tz, i * NC + c + 1)
                    dve.scalar_tensor_tensor(out=zs[:, c, :], in0=tz[:], scalar=1.0, in1=ps[:, 3, 0:256],
                                             op0=ALU.add, op1=ALU.mult).then_inc(s_zs, 1)
                    dve.wait_ge(s_aw, i * NC + c + 1)
                    if c == 0:
                        op = dve.tensor_scalar(o[:, c, :, :], ps[:, 7, 0:256].rearrange("p (e n) -> p e n", e=2),
                                               rs[:, 0, c:c + 1], None, ALU.mult)
                    else:
                        dve.wait_ge(s_qe, i * 7 + c)
                        for e in range(2):
                            op = dve.scalar_tensor_tensor(out=o[:, c, e, :], in0=ps[:, 7, e * P:(e + 1) * P], scalar=rs[:, 0, c:c + 1],
                                                          in1=qs[:, e, :], op0=ALU.mult, op1=ALU.add)
                    op.then_inc(s_o, 1)
                    while conv:
                        conv_op(i + 1, *conv.pop(0))
                for k in range(TAPS + 1):
                    conv_op(i + 1, 3, k)
                dve.wait_ge(s_rr, i * 2 + 2)
                dve.wait_ge(s_oz, i * NC + NC)
                dve.tensor_tensor(og[:], og[:], ro[:].unsqueeze(3).broadcast_to([P, NC, 2, P]), ALU.mult).then_inc(s_og, 1)
            for n in range(4):
                add_out(NK, n)
            dve.wait_ge(s_tz, NK * NC + 1)
            dve.wait_ge(s_ya, NK * 4 + 5)
            step.link(dve.scalar_tensor_tensor(out=m.yacc[:], in0=zs[:], scalar=1.0, in1=m.yacc[:], op0=ALU.add, op1=ALU.mult))
            step.link(dve.scalar_tensor_tensor(out=m.yacc[:], in0=m.yacc[:], scalar=0.5, in1=y[:], op0=ALU.mult, op1=ALU.mult))
            step.link(dve.tensor_tensor(m.x[:], m.x[:], m.yacc[:], ALU.add))


def kernel(**inputs):
    import numpy as _np
    import concourse.bacc as _bacc
    from concourse import mybir as _mybir
    from concourse.bass_utils import run_bass_kernel_spmd as _run

    a = {k: _np.asarray(v) for k, v in inputs.items()}
    packed = {
        "x": a["L0_attn_x"],
        "w_attn": _np.concatenate([a["L0_attn_wq"], a["L0_attn_wk"], a["L0_attn_wv"]], axis=1),
        "w_o": a["L0_attn_wo"],
        "gate0": a["L0_ffn_gate"],
        "gu0": a["L0_ffn_gate_up_proj"].reshape(8, 4, 2, 128, 2, 96).transpose(0, 3, 2, 4, 1, 5).reshape(8, 128, -1),
        "down0": a["L0_ffn_down_proj"].reshape(8, 3, 128, 256).transpose(0, 2, 1, 3).reshape(8, 128, -1),
        "w_conv": _key_head_groups(_np, a["L1_attn_W_qkv"]).reshape(2, 128, 17, 512).transpose(2, 1, 0, 3).reshape(17, 128, -1),
        "w_tap": _key_head_groups(_np, a["L1_attn_conv_w"].T).reshape(4, 17, 4, 128).transpose(3, 1, 2, 0).reshape(128, -1),
        "w_z": a["L1_attn_W_z"].reshape(2, 128, 16, 256).transpose(2, 1, 0, 3).reshape(16, 128, -1),
        "w_out": a["L1_attn_W_out"].reshape(16, 2, 128, 256).transpose(0, 2, 1, 3).reshape(16, 128, -1),
        "w_ba": _np.concatenate([a["L1_attn_W_b"], a["L1_attn_W_a"]], axis=1),
        "dt_bias": a["L1_attn_dt_bias"].reshape(1, 32),
        "a_log": a["L1_attn_A_log"].reshape(1, 32),
        "norm_w": a["L1_attn_norm_w"].reshape(128, 1),
        "router1": a["L1_ffn_Wr"],
        "gu1": _np.stack([a["L1_ffn_Wg"], a["L1_ffn_Wu"]]).transpose(2, 0, 1, 3).reshape(2, 128, 2, 11, 128)
                  .transpose(3, 1, 0, 2, 4).reshape(11, 128, -1),
        "down1": a["L1_ffn_Wd"].reshape(11, 128, 256),
    }
    nc = _bacc.Bacc("TRN2", target_bir_lowering=False, num_devices=1)
    arrays, args = {}, []
    for name, v in packed.items():
        v = _np.ascontiguousarray(v)
        arrays[f"in_{name}"] = v
        args.append(nc.dram_tensor(f"in_{name}", v.shape, _mybir.dt.from_np(v.dtype), kind="ExternalInput").ap())
    args.append(nc.dram_tensor("out_0", (1, 1024, 256), _mybir.dt.float32, kind="ExternalOutput").ap())
    build(nc, *args)
    r = _run(nc, [arrays], core_ids=[0])
    return r.results[0]["out_0"]


def _key_head_groups(np_, w):
    n = w.shape[0]
    q, k, v = w[:, :2048].reshape(n, 16, 128), w[:, 2048:4096].reshape(n, 16, 128), w[:, 4096:].reshape(n, 16, 256)
    g = np_.concatenate([q, k, v], axis=2)
    return np_.concatenate([g, g[:, :1]], axis=1).reshape(n, 17 * 512)
```

```python
from contextlib import ExitStack

import numpy as np

import concourse.bass as bass
from concourse import mybir

ALU = mybir.AluOpType
ACT = mybir.ActivationFunctionType
AX = mybir.AxisListType
F32 = mybir.dt.float32
BF16 = mybir.dt.bfloat16
I32 = mybir.dt.int32

P = 128
T, D = 1024, 256
NC = T // P
KT = D // P
HALF = 512
NH, NKV, HD = 32, 8, 8
REP = NH // NKV
E0, TOP0, F0 = 32, 4, 96
G0 = 4
TILES0 = G0 * F0 // P
E1, TOP1, F1 = 8, 2, 176
TILES1 = E1 * F1 // P
ESEL = 32
NV, NK, DK = 32, 16, 128
TAPS = 4
LEVELS = 7
UNITS = 2 * NC
NEG = -1e30
PAIRS = [(0, 0), (0, 1), (1, 0), (1, 1), (0, 2), (2, 0)]
QROWS = HD * len(PAIRS)
SCALE = float(HD) ** -0.5
LN_EPS = 1e-5


class Memory:
    pass


class Chain:

    def __init__(self, eng, sem, base=0):
        self.eng, self.sem, self.base, self.n = eng, sem, base, 0

    def __call__(self, instruction):
        instruction.then_inc(self.sem, 1)
        self.n += 1

    def wait(self):
        self.eng.wait_ge(self.sem, self.base + self.n)

    def link(self, instruction):
        self(instruction)
        self.wait()


def dve_layer_norm(dve, step, x, st, mv, xn, s_var, s_rstd, rstd):
    for c in range(NC):
        step(dve.bn_stats(st[:, c, :], x[:, c, :]))
    step.wait()
    for c in range(NC):
        last = dve.bn_aggr(mv[:, c, :], st[:, c, :])
    last.then_inc(s_var, 1)
    dve.wait_ge(s_var, 1)
    dve.wait_ge(s_rstd, 1)
    for c in range(NC):
        step(dve.tensor_scalar(xn[:, c, :], x[:, c, :], mv[:, c, 0:1], rstd[:, c:c + 1],
                               ALU.subtract, ALU.mult))


def pool_rsqrt_var(nc, pool, step, mv, rstd, minus_half, s_var, s_rstd):
    pool.wait_ge(s_var, 1)
    step.link(nc.gpsimd.tensor_scalar(rstd[:, 0:NC], mv[:, :, 1], LN_EPS, None, ALU.add))
    nc.gpsimd.tensor_tensor(rstd[:, 0:NC], rstd[:, 0:NC], minus_half[:, 0:1].broadcast_to([P, NC]),
                            ALU.pow).then_inc(s_rstd, 1)


def pool_expert_rows(nc, step, sel, width, experts):
    for part in range(3):
        ap = sel[ESEL * part:ESEL * part + ESEL, :]
        step.link(nc.gpsimd.affine_select(out=ap, in_=ap, compare_op=ALU.is_ge, fill=0.0, base=0,
                                          pattern=[[1, experts * width]], channel_multiplier=-width))
        step.link(nc.gpsimd.affine_select(out=ap, in_=ap, compare_op=ALU.is_ge, fill=0.0, base=width - 1,
                                          pattern=[[-1, experts * width]], channel_multiplier=width))


def dve_route(dve, step, logits, n_exp, k, rev, w, b, s_logit, s_exp, w3b, w3f):
    lg, pr, left, pick, acc = w
    r1, ix = b
    all_e = [P, NC, n_exp]

    def col(ap):
        return ap[:, :].unsqueeze(2).broadcast_to(all_e)

    step.link(dve.tensor_reduce(r1[:, :], logits, AX.X, ALU.max))
    dve.tensor_tensor(lg[:, :, 0:n_exp], logits, col(r1), ALU.subtract).then_inc(s_logit, 1)
    dve.wait_ge(s_exp, 1)
    step.link(dve.tensor_reduce(r1[:, :], pr[:, :, 0:n_exp], AX.X, ALU.add))
    step.link(dve.reciprocal(r1[:, :], r1[:, :]))
    step.link(dve.tensor_tensor(pr[:, :, 0:n_exp], pr[:, :, 0:n_exp], col(r1), ALU.mult))
    step.link(dve.tensor_copy(left[:, :, 0:n_exp], pr[:, :, 0:n_exp]))
    for n in range(k):
        step.link(dve.tensor_reduce(r1[:, :], left[:, :, 0:n_exp], AX.X, ALU.max))
        step.link(dve.tensor_tensor(pick[:, :, 0:n_exp], left[:, :, 0:n_exp], col(r1), ALU.is_equal))
        step.link(dve.tensor_tensor(pick[:, :, 0:n_exp], pick[:, :, 0:n_exp],
                                    rev[:, 0:n_exp].unsqueeze(1).broadcast_to(all_e), ALU.mult))
        step.link(dve.tensor_reduce(ix[:, :], pick[:, :, 0:n_exp], AX.X, ALU.max))
        step.link(dve.tensor_tensor(pick[:, :, 0:n_exp], pick[:, :, 0:n_exp], col(ix), ALU.is_equal))
        step.link(dve.scalar_tensor_tensor(out=left[:, :, 0:n_exp], in0=pick[:, :, 0:n_exp], scalar=-4.0,
                                           in1=left[:, :, 0:n_exp], op0=ALU.mult, op1=ALU.add))
    step.link(dve.tensor_scalar(pick[:, :, 0:n_exp], left[:, :, 0:n_exp], 0.0, None, ALU.is_lt))
    step.link(dve.tensor_tensor(acc[:, :, 0:n_exp], pick[:, :, 0:n_exp], pr[:, :, 0:n_exp], ALU.mult))
    step.link(dve.tensor_reduce(r1[:, :], acc[:, :, 0:n_exp], AX.X, ALU.add))
    step.link(dve.reciprocal(r1[:, :], r1[:, :]))
    step.link(dve.tensor_tensor(acc[:, :, 0:n_exp], acc[:, :, 0:n_exp], col(r1), ALU.mult))
    for part in range(3):
        at = slice(ESEL * part, ESEL * part + n_exp)
        step.link(dve.tensor_copy(w3b[:, :, at], acc[:, :, 0:n_exp]))
        step.link(dve.tensor_copy(w3f[:, :, at], w3b[:, :, at]))
        if part < 2:
            step.link(dve.tensor_tensor(acc[:, :, 0:n_exp], acc[:, :, 0:n_exp], w3f[:, :, at], ALU.subtract))


def build(nc, x, w_attn, w_o, gate0, gu0, down0, w_conv, w_tap, w_z, w_out, w_ba, dt_bias, a_log, norm_w,
          router1, gu1, down1, out):
    with ExitStack() as ctx:
        m = Memory()

        def sb(name, shape, dt=F32):
            return ctx.enter_context(nc.sbuf_tensor(name, shape, dt))

        m.ps = ctx.enter_context(nc.psum_tensor("ps", [P, 8, HALF], F32))
        m.x = sb("x_nat", [P, NC, D])
        m.xn = sb("xn_nat", [P, NC, D])
        m.xnT = sb("xnT", [P, KT, T])
        m.ident = sb("ident", [P, P])
        m.identb = sb("identb", [P, P], BF16)
        m.upto = sb("upto", [P, P])
        m.after = sb("after", [P, P])
        m.ones = sb("ones", [P, P])
        m.future = sb("future", [P, P], BF16)
        m.lmask = sb("lmask", [P, LEVELS, P // 2])
        m.pair_mask = sb("pair_mask", [P, P // 2, 2])
        m.minus_half = sb("minus_half", [P, 1])
        m.plus_half = sb("plus_half", [P, 1])
        m.rev = sb("rev", [P, E0])
        m.yacc = sb("yacc", [P, NC, D])
        m.st = sb("bn_st", [P, NC, 6])
        m.mv = sb("bn_mv", [P, NC, 2])
        m.rstd = sb("rstd", [P, NC])

        with ExitStack() as l0:
            def sb0(name, shape, dt=F32):
                return l0.enter_context(nc.sbuf_tensor(name, shape, dt))
            m.sel0 = sb0("sel0", [P, E0 * F0], BF16)
            m.wT3 = sb0("wT3", [P, T], BF16)
            m.qst = sb0("q_stack", [P, NH, T], BF16)
            m.kst = sb0("k_stack", [P, NKV, T], BF16)
            m.vaug = sb0("v_aug", [P, NKV, NC, 32])
            m.w_o = sb0("w_o", [P, KT, D])
            m.mpart = sb0("m_part", [P, NC, NH, 2])
            stage_inputs(nc, m, x, w_attn, w_o, gate0)
            stage_moe0_and_maxima(nc, m, gu0, down0)
            stage_attention(nc, m)
        m.beta = sb("beta", [P, NV + 2, NC])
        m.g = sb("g", [P, NV + 2, NC])
        m.eg = sb("decays", [P, 3, NV + 2, NC])
        m.neg_egc = sb("neg_egc", [P, NV + 2, NC])
        m.taps = sb("taps", [P, NK + 2, 4, TAPS])
        m.norm_w = sb("norm_w_half", [P, 1])
        with ExitStack() as l1:
            m.sel1 = l1.enter_context(nc.sbuf_tensor("sel1", [P, E1 * F1], BF16))
            m.wT3 = l1.enter_context(nc.sbuf_tensor("l1_wT3", [P, T], BF16))
            stage_l1_inputs(nc, m, router1, w_ba, dt_bias, a_log, norm_w, w_tap)
            stage_moe1(nc, m, gu1, down1)
        stage_delta(nc, m, w_conv, w_z, w_out)
        stage_store(nc, m, out)


def stage_inputs(nc, m, x, w_attn, w_o, gate0):
    with ExitStack() as ctx:
        def sb(name, shape, dt=F32):
            return ctx.enter_context(nc.sbuf_tensor(name, shape, dt))

        def sem(name):
            return ctx.enter_context(nc.semaphore(name))

        ps = m.ps
        NQ, NKC = NH * HD, NKV * HD
        wa = sb("w_attn_sb", [P, KT, NQ + 2 * NKC + E0])
        qp = sb("q_parts", [P, 3, KT, T], BF16)
        kp = sb("k_parts", [NKC, 3, T], BF16)
        rest = sb("rest", [P, 2, T])
        irev = sb("irev", [P, E0], I32)
        route = [sb(f"route{i}", [P, NC, E0]) for i in range(5)]
        route_col = [sb(f"route_col{i}", [P, NC]) for i in range(2)]
        w3b = sb("w3b", [P, NC, 3 * ESEL], BF16)
        w3f = sb("w3f", [P, NC, 3 * ESEL])
        scratch_q = nc.dram_tensor("scratch_q", [3, NQ, T], BF16).ap()
        scratch_k = nc.dram_tensor("scratch_k", [3, NKC, T], BF16).ap()
        in_x, in_w, in_wo = sem("in_x"), sem("in_w"), sem("in_wo")
        s_const, s_ident = sem("const_made"), sem("ident_made")
        s_var, s_rstd, s_xn, s_tr, s_xnT = sem("var"), sem("rstd"), sem("xn_made"), sem("xn_transposed"), sem("xnT_made")
        s_proj = sem("projected")
        s_parts = sem("parts_split")
        s_stored, s_stacked, s_zero = sem("parts_stored"), sem("stacks_loaded"), sem("stacks_zeroed")
        s_dve, s_pool = sem("dve_steps"), sem("pool_steps")
        s_logit, s_exp = sem("logits_shifted"), sem("exp_made")
        s_w3zero = sem("w3_zeroed")
        s_w3, s_wt, s_wT3 = sem("w3_split"), sem("w3_transposed"), sem("wT3_made")
        block = ctx.enter_context(nc.Block())

        @block.sync
        def _(sp):
            sp.dma_start(m.x[:], x.rearrange("b (c p) d -> p (b c) d", p=P)).then_inc(in_x, 16)
            sp.dma_start(wa[:, :, 0:NQ + 2 * NKC], w_attn.rearrange("(k p) n -> p k n", p=P)).then_inc(in_w, 16)
            sp.dma_start(wa[:, :, NQ + 2 * NKC:], gate0.rearrange("(k p) n -> p k n", p=P)).then_inc(in_w, 16)
            sp.dma_start(m.w_o[:], w_o.rearrange("(k p) n -> p k n", p=P)).then_inc(in_wo, 16)
            sp.wait_ge(s_parts, 3)
            sp.dma_start(scratch_k.rearrange("s c t -> c s t"), kp[:]).then_inc(s_stored, 16)
            for k in range(KT):
                for part in range(3):
                    sp.dma_start(scratch_q[part, k * P:(k + 1) * P, :], qp[:, part, k, :]).then_inc(s_stored, 16)
            sp.wait_ge(s_stored, 16 * 7)
            sp.wait_ge(s_zero, 2)
            for r, (a, b) in enumerate(PAIRS):
                rows = slice(HD * r, HD * (r + 1))
                sp.dma_start(m.qst[rows, :, :], scratch_q[a].rearrange("(h d) t -> d h t", d=HD)).then_inc(s_stacked, 16)
                sp.dma_start(m.kst[rows, :, :], scratch_k[b].rearrange("(h d) t -> d h t", d=HD)).then_inc(s_stacked, 16)
            sp.wait_ge(s_stacked, 32 * len(PAIRS))
            sp.wait_ge(in_wo, 16)

        @block.gpsimd
        def _(pool):
            step = Chain(pool, s_pool)
            g = nc.gpsimd

            def select(ap, op, base, pattern, cm, fill):
                step.link(g.affine_select(out=ap, in_=ap, compare_op=op, fill=fill, base=base,
                                          pattern=pattern, channel_multiplier=cm))
            step(g.memset(m.minus_half[:], -0.5))
            step(g.memset(m.plus_half[:], 0.5))
            step.link(g.memset(m.ident[:], 0.0))
            select(m.ident[:], ALU.not_equal, 0, [[-1, P]], 1, 1.0)
            g.tensor_copy(m.identb[:], m.ident[:]).then_inc(s_ident, 1)
            pool_rsqrt_var(nc, pool, step, m.mv, m.rstd, m.minus_half, s_var, s_rstd)
            step(g.memset(m.mpart[:], NEG))
            step(g.iota(irev[:], pattern=[[-1, E0]], base=E0, channel_multiplier=0))
            step(g.memset(m.upto[:], 1.0))
            step(g.memset(m.after[:], 1.0))
            step(g.memset(m.ones[:], 1.0))
            step(g.memset(m.future[:], 0.0))
            step(g.memset(m.lmask[:], 1.0))
            step(g.memset(m.pair_mask[:], 0.0))
            step(g.memset(m.sel0[:], 1.0))
            step.wait()
            step(g.tensor_copy(m.rev[:], irev[:]))
            step.link(g.memset(m.kst[:], 0.0))
            step.link(g.memset(m.kst[32:64, :, :], 1.0))
            select(m.kst[32:64, :, :], ALU.is_ge, QROWS + 2 - 32, [[0, NKV], [0, T]], -1, 0.0)
            pool.sem_inc(s_zero, 1)
            g.memset(w3f[:], 0.0).then_inc(s_w3zero, 1)
            select(m.upto[:], ALU.is_ge, 0, [[1, P]], -1, 0.0)
            select(m.after[:], ALU.is_ge, -1, [[-1, P]], 1, 0.0)
            select(m.future[:], ALU.is_ge, 0, [[1, P]], -1, NEG)
            select(m.pair_mask[:, :, 1], ALU.not_equal, 0, [[-2, P // 2]], 1, -1.0)
            for lv in range(LEVELS):
                s = 1 << lv
                ap = m.lmask[:, lv, :].rearrange("p (b s) -> p b s", s=s)
                select(ap, ALU.is_ge, -s, [[-2 * s, P // (2 * s)], [0, s]], 1, 0.0)
                select(ap, ALU.is_ge, 2 * s - 1, [[2 * s, P // (2 * s)], [0, s]], -1, 0.0)
            pool_expert_rows(nc, step, m.sel0, F0, E0)

        @block.vector
        def _(dve):
            step = Chain(dve, s_dve)
            dve.wait_ge(in_x, 16)
            dve_layer_norm(dve, step, m.x, m.st, m.mv, m.xn, s_var, s_rstd, m.rstd)
            step.wait()
            dve.memset(m.qst[:], 0.0).then_inc(s_zero, 1)
            step.link(dve.memset(m.vaug[:], 0.0))
            step.link(dve.memset(m.vaug[:, :, :, HD:HD + 1], 1.0))
            for n in range(3):
                dve.wait_ge(s_proj, n + 1)
                rows = P if n < 2 else NKC
                banks = slice(4 + 2 * n, 6 + 2 * n) if n < 2 else slice(0, 2)
                src = ps[0:rows, banks, :].rearrange("p b n -> p (b n)")
                parts = [qp[:, s, n, :] if n < 2 else kp[:, s, :] for s in range(3)]
                step.link(dve.tensor_copy(parts[0], src))
                step.link(dve.tensor_tensor(rest[0:rows, 0, :], src, parts[0], ALU.subtract))
                step.link(dve.tensor_copy(parts[1], rest[0:rows, 0, :]))
                dve.tensor_tensor(parts[2], rest[0:rows, 0, :], parts[1], ALU.subtract).then_inc(s_parts, 1)
                dve.wait_ge(s_parts, n + 1)
            dve.wait_ge(s_proj, 4)
            step(dve.tensor_copy(m.vaug[:, :, :, 0:HD].rearrange("p g c d -> p c g d"),
                                 ps[:, 2, :].rearrange("p (c g d) -> p c g d", c=NC, d=HD)))
            dve.wait_ge(s_proj, 5)
            dve.wait_ge(s_w3zero, 1)
            dve_route(dve, step, ps[:, 3, 0:NC * E0].rearrange("p (c e) -> p c e", e=E0), E0, TOP0, m.rev,
                      route, route_col, s_logit, s_exp, w3b, w3f)
            dve.sem_inc(s_w3, 1)

        @block.tensor
        def _(pe):
            pe.wait_ge(s_ident, 1)
            pe.wait_ge(s_dve, 2 * NC)
            for k in range(KT):
                for c in range(NC):
                    mm = pe.transpose(ps[:, 2 * k + c // 4, (c % 4) * P:(c % 4 + 1) * P],
                                      m.xn[:, c, k * P:(k + 1) * P], m.ident[:])
                mm.then_inc(s_tr, 1)
            pe.wait_ge(in_w, 32)
            pe.wait_ge(s_xnT, 2)
            for n in range(2):
                for h in range(2):
                    for k in range(KT):
                        mm = pe.matmul(ps[:, 4 + 2 * n + h, :], wa[:, k, n * P:(n + 1) * P],
                                       m.xnT[:, k, h * HALF:(h + 1) * HALF], start=k == 0, stop=k == KT - 1)
                mm.then_inc(s_proj, 1)
            for h in range(2):
                for k in range(KT):
                    mm = pe.matmul(ps[0:NKC, h, :], wa[:, k, NQ:NQ + NKC],
                                   m.xnT[:, k, h * HALF:(h + 1) * HALF], start=k == 0, stop=k == KT - 1)
            mm.then_inc(s_proj, 1)
            for bank, a, n in ((2, NQ + NKC, NKC), (3, NQ + 2 * NKC, E0)):
                for c in range(NC):
                    for k in range(KT):
                        mm = pe.matmul(ps[:, bank, c * n:(c + 1) * n], m.xnT[:, k, c * P:(c + 1) * P],
                                       wa[:, k, a:a + n], start=k == 0, stop=k == KT - 1)
                mm.then_inc(s_proj, 1)
            pe.wait_ge(s_w3, 1)
            pe.wait_ge(s_parts, 3)
            for c in range(NC):
                mm = pe.transpose(ps[0:3 * ESEL, c // 4, (c % 4) * P:(c % 4 + 1) * P], w3f[:, c, :], m.ident[:])
            mm.then_inc(s_wt, 1)

        @block.scalar
        def _(act):
            for k in range(KT):
                act.wait_ge(s_tr, k + 1)
                nc.scalar.copy(m.xnT[:, k, :], ps[:, 2 * k:2 * k + 2, :].rearrange("p b n -> p (b n)")).then_inc(s_xnT, 1)
            act.wait_ge(s_logit, 1)
            nc.scalar.activation(route[1][:], route[0][:], ACT.Exp).then_inc(s_exp, 1)
            act.wait_ge(s_wt, 1)
            nc.scalar.copy(m.wT3[0:3 * ESEL, :], ps[0:3 * ESEL, 0:2, :].rearrange("p b n -> p (b n)")).then_inc(s_wT3, 1)
            act.wait_ge(s_wT3, 1)


def stage_moe0_and_maxima(nc, m, gu0, down0):
    PASSES = E0 // G0
    FW = G0 * F0
    SBANKS = REP * 12
    NJ = 2 * TILES0
    with ExitStack() as ctx:
        def sb(name, shape, dt=F32):
            return ctx.enter_context(nc.sbuf_tensor(name, shape, dt))

        def sem(name):
            return ctx.enter_context(nc.semaphore(name))

        ps = m.ps
        wgu = sb("w_gate_up", [P, KT, 2, FW])
        wd = sb("w_down", [P, TILES0, D])
        th = sb("tanh_g", [P, 2, HALF])
        hid = sb("hidden", [P, TILES0, T])
        gs = sb("gate_silu", [P, 2, HALF])
        neg_m = sb("neg_m", [P, NC, NH])
        m3f = sb("m3f", [P, NC, 3, NH])
        m3b = sb("m3b", [P, NC, 3, NH], BF16)
        mT3 = sb("mT3", [3 * NH, T], BF16)
        scratch_m = nc.dram_tensor("scratch_m", [3, NH, T], BF16).ap()
        s_wgu, s_wd = sem("w_gate_up_in"), sem("w_down_in")
        s_gu, s_w, s_th = sem("gate_up_made"), sem("weight_row_made"), sem("tanh_made")
        s_gs, s_hu, s_h = sem("gate_silu_made"), sem("hidden_unscaled"), sem("hidden_made")
        s_dn, s_y = sem("down_made"), sem("down_added")
        s_sc, s_max = sem("scores_made"), sem("scores_maxed")
        s_dve, s_mt, s_mT3 = sem("dve_steps"), sem("m_transposed"), sem("mT3_made")
        s_mst, s_mld = sem("m_stored"), sem("m_stacked")
        block = ctx.enter_context(nc.Block())

        def score_banks(hh):
            for qt in range(NC):
                keys = (qt + 1) * P
                for half in range((keys + HALF - 1) // HALF):
                    yield qt, half, min(HALF, keys - half * HALF)

        @block.sync
        def _(sp):
            with sp.Fori(0, PASSES) as i:
                sp.wait_ge(s_gu, i * NJ + 1)
                sp.dma_start(wgu[:].rearrange("p k g n -> p (k g n)"), gu0[bass.ds(i, 1)].rearrange("i p n -> (i p) n")).then_inc(s_wgu, 16)
                sp.wait_ge(s_dn, i * 4 + 1)
                sp.dma_start(wd[:].rearrange("p t n -> p (t n)"), down0[bass.ds(i, 1)].rearrange("i p n -> (i p) n")).then_inc(s_wd, 16)
            sp.wait_ge(s_mT3, 1)
            sp.dma_start(scratch_m.rearrange("s h t -> (s h) t"), mT3[:]).then_inc(s_mst, 16)
            sp.wait_ge(s_mst, 16)
            sp.dma_start(m.qst[QROWS:QROWS + 3, :, :], scratch_m).then_inc(s_mld, 16)
            sp.wait_ge(s_mld, 16)

        @block.tensor
        def _(pe):
            pe.sem_inc(s_gu, 1)
            pe.sem_inc(s_dn, 1)
            with pe.Fori(0, PASSES) as i:
                n_bank = 0
                order = [(hh, b) for hh in range(REP) for b in score_banks(hh)]

                def score_bank():
                    nonlocal n_bank
                    hh, (qt, half, cols) = order[n_bank]
                    bank = 6 + n_bank % 2
                    pe.wait_ge(s_max, i * SBANKS + n_bank + 1)
                    diag = half * HALF + cols == (qt + 1) * P
                    mm = pe.matmul(ps[:, bank, 0:cols], m.qst[:, bass.ds(i * REP + hh, 1), qt * P:(qt + 1) * P],
                                   m.kst[:, bass.ds(i, 1), half * HALF:half * HALF + cols],
                                   start=True, stop=not diag)
                    if diag:
                        mm = pe.matmul(ps[:, bank, cols - P:cols], m.future[:], m.identb[:], start=False, stop=True)
                    mm.then_inc(s_sc, 1)
                    n_bank += 1

                pe.wait_ge(s_wgu, i * 16 + 16)
                for j in range(NJ):
                    tile, half = j // 2, j % 2
                    cols = slice(half * HALF, (half + 1) * HALF)
                    gb = 2 * (j % 2)
                    pe.wait_ge(s_hu, i * NJ + j + 1)
                    for which in range(2):
                        for k in range(KT):
                            mm = pe.matmul(ps[:, gb + which, :], wgu[:, k, which, tile * P:(tile + 1) * P],
                                           m.xnT[:, k, cols], start=k == 0, stop=k == KT - 1)
                            if which == 1 and k == KT - 1:
                                mm.then_inc(s_gu, 1)
                            score_bank()
                    pe.wait_ge(s_h, i * NJ + j + 1)
                    if j == 0:
                        pe.wait_ge(s_y, i * 4 + 2)
                    pe.matmul(ps[:, 4, :], m.sel0[0:3 * ESEL, bass.ds(i * FW + tile * P, P)], m.wT3[0:3 * ESEL, cols],
                              start=True, stop=True).then_inc(s_w, 1)
                    score_bank()
                pe.wait_ge(s_wd, i * 16 + 16)
                for _ in range(2):
                    score_bank()
                for c2 in range(NC // 2):
                    if c2 < 2:
                        pe.wait_ge(s_h, i * NJ + NJ + c2)
                    pe.wait_ge(s_y, i * 4 + c2 + 1)
                    for c in (2 * c2, 2 * c2 + 1):
                        for t in range(TILES0):
                            mm = pe.matmul(ps[:, 5 - c2 % 2, (c % 2) * D:(c % 2 + 1) * D], hid[:, t, c * P:(c + 1) * P], wd[:, t, :],
                                           start=t == 0, stop=t == TILES0 - 1)
                            if c == 2 * c2 + 1 and t == TILES0 - 1:
                                mm.then_inc(s_dn, 1)
                            if t < 2:
                                score_bank()
                assert n_bank == SBANKS
            pe.wait_ge(s_dve, 100)
            for c in range(NC):
                mm = pe.transpose(ps[0:3 * NH, c // 4, (c % 4) * P:(c % 4 + 1) * P],
                                  m3f[:, c, :, :].rearrange("p s h -> p (s h)"), m.ident[:])
            mm.then_inc(s_mt, 1)

        @block.scalar
        def _(act):
            with act.Fori(0, PASSES) as i:
                for j in range(NJ):
                    act.wait_ge(s_gu, i * NJ + j + 2)
                    act.wait_ge(s_gs, i * NJ + j + 1)
                    nc.scalar.activation(th[:, j % 2, :], ps[:, 2 * (j % 2), :], ACT.Tanh, scale=0.5).then_inc(s_th, 1)
            act.wait_ge(s_mt, 1)
            nc.scalar.copy(mT3[:], ps[0:3 * NH, 0:2, :].rearrange("p b n -> p (b n)")).then_inc(s_mT3, 1)

        @block.vector
        def _(dve):
            step = Chain(dve, s_dve)
            step.link(dve.memset(m.yacc[:], 0.0))
            dve.sem_inc(s_max, 2)
            dve.sem_inc(s_hu, 2)
            dve.sem_inc(s_gs, 2)
            dve.sem_inc(s_h, 1)
            dve.sem_inc(s_y, 2)
            with dve.Fori(0, PASSES) as i:
                order = [(hh, b) for hh in range(REP) for b in score_banks(hh)]
                n_bank = 0

                def maximum():
                    nonlocal n_bank
                    hh, (qt, half, cols) = order[n_bank]
                    dve.wait_ge(s_sc, i * SBANKS + n_bank + 1)
                    dve.tensor_reduce(m.mpart[:, qt, bass.ds(i * REP + hh, 1), half:half + 1], ps[:, 6 + n_bank % 2, 0:cols],
                                      AX.X, ALU.max).then_inc(s_max, 1)
                    n_bank += 1

                def hidden(j):
                    tile, half = j // 2, j % 2
                    cols = slice(half * HALF, (half + 1) * HALF)
                    dve.wait_ge(s_th, i * NJ + j + 1)
                    dve.scalar_tensor_tensor(out=gs[:, j % 2, :], in0=th[:, j % 2, :], scalar=1.0, in1=ps[:, 2 * (j % 2), :],
                                             op0=ALU.add, op1=ALU.mult).then_inc(s_gs, 1)
                    if j < NJ - 1:
                        maximum()
                    dve.wait_ge(s_gs, i * NJ + j + 3)
                    if j == 0:
                        dve.wait_ge(s_dn, i * 4 + 1)
                    dve.scalar_tensor_tensor(out=hid[:, tile, cols], in0=gs[:, j % 2, :], scalar=0.5,
                                             in1=ps[:, 2 * (j % 2) + 1, :], op0=ALU.mult, op1=ALU.mult).then_inc(s_hu, 1)
                    if j < NJ - 1:
                        maximum()
                    dve.wait_ge(s_hu, i * NJ + j + 3)
                    dve.wait_ge(s_w, i * NJ + j + 1)
                    dve.tensor_tensor(hid[:, tile, cols], hid[:, tile, cols], ps[:, 4, :], ALU.mult).then_inc(s_h, 1)

                for j in range(NJ):
                    maximum()
                    if j:
                        hidden(j - 1)
                        maximum()
                        maximum()
                    else:
                        for _ in range(4):
                            maximum()
                hidden(NJ - 1)
                maximum()
                maximum()
                for c2 in range(NC // 2):
                    maximum()
                    maximum()
                    maximum()
                    dve.wait_ge(s_dn, i * 4 + c2 + 2)
                    dve.tensor_tensor(m.yacc[:, 2 * c2:2 * c2 + 2, :], m.yacc[:, 2 * c2:2 * c2 + 2, :],
                                      ps[:, 5 - c2 % 2, :].rearrange("p (c d) -> p c d", c=2), ALU.add).then_inc(s_y, 1)
                    maximum()
                assert n_bank == SBANKS
            dve.wait_ge(s_max, PASSES * SBANKS + 2)
            step.link(dve.tensor_tensor(neg_m[:, :, :], m.mpart[:, :, :, 0], m.mpart[:, :, :, 1], ALU.max))
            step.link(dve.tensor_scalar(neg_m[:], neg_m[:], -1.0, None, ALU.mult))
            for part in range(3):
                step.link(dve.tensor_copy(m3b[:, :, part, :], neg_m[:]))
                step.link(dve.tensor_copy(m3f[:, :, part, :], m3b[:, :, part, :]))
                if part < 2:
                    step.link(dve.tensor_tensor(neg_m[:], neg_m[:], m3f[:, :, part, :], ALU.subtract))
            dve.sem_inc(s_dve, 100)


def stage_attention(nc, m):
    with ExitStack() as ctx:
        def sb(name, shape, dt=F32):
            return ctx.enter_context(nc.sbuf_tensor(name, shape, dt))

        def sem(name):
            return ctx.enter_context(nc.semaphore(name))

        ps = m.ps
        m.oT = sb("oT", [P, NKV, T])
        vst = sb("v_stage", [P, NC, 32])
        pr = sb("probs", [P, 2, REP, T])
        w_yn = m.xn
        inv = sb("inv_sum", [P, NC, NH])
        yT = m.xnT
        tanh_y = m.oT[:, 0:2, :].rearrange("p g (c d) -> p (g c) d", d=D)
        s_v, s_sc, s_pr, s_pv, s_o = sem("v_staged"), sem("scores_made"), sem("probs_made"), sem("pv_made"), sem("o_copied")
        s_ot, s_inv, s_yn, s_yt, s_yT, s_s, s_dve = (sem("o_transposed"), sem("inv_made"), sem("y_normed"), sem("y_transposed"),
                                              sem("yT_made"), sem("s_made"), sem("dve_steps"))
        block = ctx.enter_context(nc.Block())
        UN = NC * REP

        @block.tensor
        def _(pe):
            pe.sem_inc(s_pv, 2)
            with pe.Fori(0, NKV) as i:
                def pv(kt):
                    pe.wait_ge(s_pr, i * UN + REP * (kt + 1) + 3)
                    if kt == 0:
                        pe.wait_ge(s_v, i + 1)
                        pe.wait_ge(s_o, i + 1)
                    for half in range(2):
                        lo = max(kt * P, half * HALF)
                        hi = (half + 1) * HALF
                        if lo >= hi:
                            continue
                        for h in range(REP):
                            mm = pe.matmul(ps[32 * h:32 * h + 32, 6 + half, lo - half * HALF:HALF], vst[:, kt, :],
                                           pr[:, kt % 2, h, lo - kt * P:hi - kt * P], start=kt == 0, stop=kt == 4 * half + 3)
                    mm.then_inc(s_pv, 1)

                for kt in range(NC):
                    cols = T - kt * P
                    for h in range(REP):
                        n = kt * REP + h
                        b0 = 2 * (n % 3)
                        pe.wait_ge(s_pr, i * UN + n + 1)
                        done = 0
                        while done < cols:
                            w = min(HALF, cols - done)
                            mm = pe.matmul(ps[:, b0 + done // HALF, 0:w], m.kst[:, bass.ds(i, 1), kt * P:(kt + 1) * P],
                                           m.qst[:, bass.ds(i * REP + h, 1), kt * P + done:kt * P + done + w],
                                           start=True, stop=done > 0)
                            if done == 0:
                                mm = pe.matmul(ps[:, b0, 0:P], m.identb[:], m.future[:], start=False, stop=True)
                            done += w
                        mm.then_inc(s_sc, 1)
                    if kt:
                        pv(kt - 1)
                pv(NC - 1)
            for c in range(NC):
                b0 = 2 * (c % 2)
                if c == 0:
                    pe.wait_ge(s_o, NKV + 1)
                if c >= 2:
                    pe.wait_ge(s_yn, c - 1)
                for g in range(NKV):
                    mm = pe.transpose(ps[:, b0 + g // 4, (g % 4) * P:(g % 4 + 1) * P], m.oT[:, g, c * P:(c + 1) * P], m.ident[:])
                mm.then_inc(s_ot, 1)
            pe.wait_ge(s_yn, NC)
            for k in range(KT):
                for c in range(NC):
                    mm = pe.transpose(ps[:, 4 + 2 * k + c // 4, (c % 4) * P:(c % 4 + 1) * P],
                                      w_yn[:, c, k * P:(k + 1) * P], m.ident[:])
            mm.then_inc(s_yt, 1)
            pe.wait_ge(s_yT, 1)
            for c in range(NC):
                for k in range(KT):
                    mm = pe.matmul(ps[:, c // 2, (c % 2) * D:(c % 2 + 1) * D], yT[:, k, c * P:(c + 1) * P], m.w_o[:, k, :],
                                   start=k == 0, stop=k == KT - 1)
            mm.then_inc(s_s, 1)

        @block.scalar
        def _(act):
            act.sem_inc(s_pr, 3)
            with act.Fori(0, NKV) as i:
                for kt in range(NC):
                    cols = T - kt * P
                    act.wait_ge(s_pv, i * NC + kt + 1)
                    for h in range(REP):
                        n = kt * REP + h
                        act.wait_ge(s_sc, i * UN + n + 1)
                        nc.scalar.activation(pr[:, kt % 2, h, 0:cols],
                                             ps[:, 2 * (n % 3):2 * (n % 3) + 2, :].rearrange("p b n -> p (b n)")[:, 0:cols],
                                             ACT.Exp, scale=SCALE).then_inc(s_pr, 1)
            act.wait_ge(s_yt, 1)
            nc.scalar.copy(yT[:].rearrange("p k t -> p (k t)"), ps[:, 4:8, :].rearrange("p b n -> p (b n)")).then_inc(s_yT, 1)
            nc.scalar.activation(tanh_y, m.yacc[:], ACT.Tanh, scale=0.5).then_inc(s_inv, 1)

        @block.vector
        def _(dve):
            step = Chain(dve, s_dve)
            dve.sem_inc(s_o, 1)
            with dve.Fori(0, NKV) as i:
                dve.wait_ge(s_pv, i * NC + 2)
                dve.tensor_copy(vst[:], m.vaug[:, bass.ds(i, 1), :, :].rearrange("p g c d -> p (g c) d")).then_inc(s_v, 1)
                dve.wait_ge(s_pv, (i + 1) * NC + 2)
                dve.tensor_copy(m.oT[:, bass.ds(i, 1), :].rearrange("p g t -> p (g t)"),
                                ps[:, 6:8, :].rearrange("p b n -> p (b n)")).then_inc(s_o, 1)
            for c in range(NC):
                dve.wait_ge(s_ot, c + 1)
                src = ps[:, 2 * (c % 2):2 * (c % 2) + 2, :].rearrange("p b (g d) -> p (b g) d", d=32)
                step.link(dve.reciprocal(inv[:, c, :], src[:, :, HD]))
                dve.tensor_tensor(w_yn[:, c, :].rearrange("p (h d) -> p h d", d=HD), src[:, :, 0:HD],
                                  inv[:, c, :].unsqueeze(2).broadcast_to([P, NH, HD]), ALU.mult).then_inc(s_yn, 1)
            dve.wait_ge(s_inv, 1)
            step.link(dve.scalar_tensor_tensor(out=m.yacc[:], in0=tanh_y, scalar=1.0, in1=m.yacc[:], op0=ALU.add, op1=ALU.mult))
            dve.wait_ge(s_s, 1)
            src = ps[:, 0:4, :].rearrange("p b (c d) -> p (b c) d", d=D)
            step.link(dve.scalar_tensor_tensor(out=m.yacc[:], in0=m.yacc[:], scalar=0.5, in1=src, op0=ALU.mult, op1=ALU.mult))
            step.link(dve.tensor_tensor(m.x[:], m.x[:], m.yacc[:], ALU.add))


def stage_store(nc, m, out):
    with ExitStack() as ctx:
        s_out = ctx.enter_context(nc.semaphore("out_stored"))
        block = ctx.enter_context(nc.Block())

        @block.sync
        def _(sp):
            sp.dma_start(out.rearrange("b (c p) d -> p (b c) d", p=P), m.x[:]).then_inc(s_out, 16)
            sp.wait_ge(s_out, 16)


def stage_l1_inputs(nc, m, router1, w_ba, dt_bias, a_log, norm_w, w_tap):
    with ExitStack() as ctx:
        def sb(name, shape, dt=F32):
            return ctx.enter_context(nc.sbuf_tensor("l1_" + name, shape, dt))

        def sem(name):
            return ctx.enter_context(nc.semaphore(name))

        ps = m.ps
        wr = sb("w_small", [P, KT, E1 + 2 * NV])
        dtb = sb("dt_b", [P, NV])
        alg = sb("a_log_b", [P, NV])
        nw = sb("norm_w_in", [P, 1])
        tap = sb("tap_in", [P, NK + 1, 4, TAPS])
        route = [sb(f"route{i}", [P, NC, E0]) for i in range(5)]
        route_col = [sb(f"route_col{i}", [P, NC]) for i in range(2)]
        w3b = sb("w3b", [P, NC, 3 * ESEL], BF16)
        w3f = sb("w3f", [P, NC, 3 * ESEL])
        za, ea, sa, s2, pol = (sb(f"gate_t{i}", [P, NV, NC]) for i in range(5))
        in_w = sem("small_in")
        s_var, s_rstd, s_tr, s_xnT, s_proj = sem("var"), sem("rstd"), sem("xn_transposed"), sem("xnT_made"), sem("projected")
        s_dve, s_pool, s_zero = sem("dve_steps"), sem("pool_steps"), sem("w3_zeroed")
        s_logit, s_exp, s_w3, s_wt, s_wT3 = (sem("logits_shifted"), sem("exp_made"), sem("w3_split"), sem("w3_transposed"),
                                             sem("wT3_made"))
        s_ab, s_eab, s_g, s_gc, s_eg, s_neg = (sem("ab_shifted"), sem("ab_exped"), sem("g_made"), sem("g_summed"),
                                        sem("decays_made"), sem("decays_negated"))
        block = ctx.enter_context(nc.Block())

        @block.sync
        def _(sp):
            sp.dma_start(wr[:, :, 0:E1], router1.rearrange("(k p) n -> p k n", p=P)).then_inc(in_w, 16)
            sp.dma_start(wr[:, :, E1:], w_ba.rearrange("(k p) n -> p k n", p=P)).then_inc(in_w, 16)
            sp.dma_start(dtb[:], dt_bias.broadcast_to([P, NV])).then_inc(in_w, 16)
            sp.dma_start(alg[:], a_log.broadcast_to([P, NV])).then_inc(in_w, 16)
            sp.dma_start(nw[:], norm_w).then_inc(in_w, 16)
            sp.dma_start(tap[:].rearrange("p a b c -> p (a b c)"), w_tap).then_inc(in_w, 16)

        @block.gpsimd
        def _(pool):
            step = Chain(pool, s_pool)
            nc.gpsimd.memset(w3f[:], 0.0).then_inc(s_zero, 1)
            pool_rsqrt_var(nc, pool, step, m.mv, m.rstd, m.minus_half, s_var, s_rstd)
            step.link(nc.gpsimd.memset(m.sel1[:], 1.0))
            pool_expert_rows(nc, step, m.sel1, F1, E1)

        @block.tensor
        def _(pe):
            pe.wait_ge(s_dve, 2 * NC)
            for k in range(KT):
                for c in range(NC):
                    mm = pe.transpose(ps[:, 2 * k + c // 4, (c % 4) * P:(c % 4 + 1) * P],
                                      m.xn[:, c, k * P:(k + 1) * P], m.ident[:])
                mm.then_inc(s_tr, 1)
            pe.wait_ge(in_w, 96)
            pe.wait_ge(s_xnT, 2)
            for bank, a, n in ((4, 0, E1), (5, E1, 2 * NV)):
                for c in range(NC):
                    for k in range(KT):
                        mm = pe.matmul(ps[:, bank, c * n:(c + 1) * n], m.xnT[:, k, c * P:(c + 1) * P],
                                       wr[:, k, a:a + n], start=k == 0, stop=k == KT - 1)
                mm.then_inc(s_proj, 1)
            pe.wait_ge(s_g, 1)
            gall = m.g[:, 0:NV, :].rearrange("p h c -> p (h c)")
            pe.matmul(ps[:, 6, 0:NV * NC], m.upto[:], gall, start=True, stop=True)
            pe.matmul(ps[:, 6, NV * NC:], m.after[:], gall, start=True, stop=True)
            pe.matmul(ps[:, 7, 0:NV * NC], m.ones[:], gall, start=True, stop=True).then_inc(s_gc, 1)
            pe.wait_ge(s_w3, 1)
            for c in range(NC):
                mm = pe.transpose(ps[0:3 * ESEL, c // 4, (c % 4) * P:(c % 4 + 1) * P], w3f[:, c, :], m.ident[:])
            mm.then_inc(s_wt, 1)

        @block.scalar
        def _(act):
            for k in range(KT):
                act.wait_ge(s_tr, k + 1)
                nc.scalar.copy(m.xnT[:, k, :], ps[:, 2 * k:2 * k + 2, :].rearrange("p b n -> p (b n)")).then_inc(s_xnT, 1)
            act.wait_ge(s_ab, 1)
            nc.scalar.activation(m.beta[:, 0:NV, :], m.beta[:, 0:NV, :], ACT.Exp, scale=-1.0).then_inc(s_eab, 1)
            nc.scalar.activation(ea[:], sa[:], ACT.Exp).then_inc(s_eab, 1)
            nc.scalar.activation(alg[:], alg[:], ACT.Exp).then_inc(s_eab, 1)
            act.wait_ge(s_gc, 1)
            for n, src in enumerate((ps[:, 6, 0:NV * NC], ps[:, 6, NV * NC:], ps[:, 7, 0:NV * NC])):
                nc.scalar.activation(m.eg[:, n, 0:NV, :].rearrange("p h c -> p (h c)"), src, ACT.Exp).then_inc(s_eg, 1)
            act.wait_ge(s_logit, 1)
            nc.scalar.activation(route[1][:, :, 0:E1], route[0][:, :, 0:E1], ACT.Exp).then_inc(s_exp, 1)
            act.wait_ge(s_wt, 1)
            nc.scalar.copy(m.wT3[0:3 * ESEL, :], ps[0:3 * ESEL, 0:2, :].rearrange("p b n -> p (b n)")).then_inc(s_wT3, 1)

        @block.vector
        def _(dve):
            step = Chain(dve, s_dve)
            dve_layer_norm(dve, step, m.x, m.st, m.mv, m.xn, s_var, s_rstd, m.rstd)
            dve.wait_ge(in_w, 96)
            step.link(dve.tensor_scalar(m.norm_w[:], nw[:], 0.5, None, ALU.mult))
            step.link(dve.tensor_scalar(m.taps[:, 0:NK + 1], tap[:], 0.5, None, ALU.mult))
            step.link(dve.tensor_scalar(m.taps[:, NK + 1:], tap[:, 0:1], 0.5, None, ALU.mult))
            dve.wait_ge(s_proj, 2)
            ba = ps[:, 5, :].rearrange("p (c n) -> p n c", c=NC)
            full = [P, NV, NC]
            beta, g = m.beta[:, 0:NV, :], m.g[:, 0:NV, :]
            step.link(dve.tensor_copy(beta, ba[:, 0:NV, :]))
            step.link(dve.tensor_tensor(za[:], ba[:, NV:, :], dtb[:].unsqueeze(2).broadcast_to(full), ALU.add))
            step.link(dve.scalar_tensor_tensor(out=sa[:], in0=za[:], scalar=-1.0, in1=za[:], op0=ALU.mult, op1=ALU.min))
            dve.sem_inc(s_ab, 1)
            dve.wait_ge(s_eab, 3)
            step.link(dve.tensor_scalar(beta, beta, 1.0, None, ALU.add))
            step.link(dve.reciprocal(beta, beta))
            step.link(dve.tensor_copy(m.beta[:, NV:, :], m.beta[:, 0:2, :]))
            step.link(dve.tensor_scalar(sa[:], ea[:], 2.0, None, ALU.add))
            step.link(dve.reciprocal(sa[:], sa[:]))
            step.link(dve.tensor_tensor(sa[:], sa[:], ea[:], ALU.mult))
            step.link(dve.tensor_tensor(s2[:], sa[:], sa[:], ALU.mult))
            step.link(dve.tensor_scalar(pol[:], s2[:], 1.0 / 15, 1.0 / 13, ALU.mult, ALU.add))
            for n in (11, 9, 7, 5, 3, 1):
                step.link(dve.tensor_tensor(pol[:], pol[:], s2[:], ALU.mult))
                step.link(dve.tensor_scalar(pol[:], pol[:], 1.0 / n, None, ALU.add))
            step.link(dve.scalar_tensor_tensor(out=pol[:], in0=pol[:], scalar=2.0, in1=sa[:], op0=ALU.mult, op1=ALU.mult))
            step.link(dve.scalar_tensor_tensor(out=pol[:], in0=za[:], scalar=0.0, in1=pol[:], op0=ALU.max, op1=ALU.add))
            step.link(dve.tensor_tensor(pol[:], pol[:], alg[:].unsqueeze(2).broadcast_to(full), ALU.mult))
            step.link(dve.tensor_scalar(g, pol[:], -1.0, -110.0, ALU.mult, ALU.max))
            dve.tensor_copy(m.g[:, NV:, :], m.g[:, 0:2, :]).then_inc(s_g, 1)
            dve.wait_ge(s_zero, 1)
            dve_route(dve, step, ps[:, 4, 0:NC * E1].rearrange("p (c e) -> p c e", e=E1), E1, TOP1, m.rev,
                      route, route_col, s_logit, s_exp, w3b, w3f)
            dve.sem_inc(s_w3, 1)
            dve.wait_ge(s_eg, 3)
            step.link(dve.tensor_copy(m.eg[:, :, NV:, :], m.eg[:, :, 0:2, :]))
            step.link(dve.tensor_scalar(m.neg_egc[:, :, :], m.eg[:, 0, :, :], -1.0, None, ALU.mult))


def stage_moe1(nc, m, gu1, down1):
    with ExitStack() as ctx:
        def sb(name, shape, dt=F32):
            return ctx.enter_context(nc.sbuf_tensor("l1_" + name, shape, dt))

        def sem(name):
            return ctx.enter_context(nc.semaphore(name))

        ps = m.ps
        wgu = sb("w_gate_up", [P, KT, 2, P])
        wd = sb("w_down", [P, D])
        th = sb("tanh_g", [P, 2, HALF])
        hid = sb("hidden", [P, T])
        gs = sb("gate_silu", [P, 2, HALF])
        s_wgu, s_wd = sem("w_gate_up_in"), sem("w_down_in")
        s_gu, s_w, s_th = sem("gate_up_made"), sem("weight_row_made"), sem("tanh_made")
        s_gs, s_hu, s_h = sem("gate_silu_made"), sem("hidden_unscaled"), sem("hidden_made")
        s_dn, s_y, s_dve = sem("down_made"), sem("down_added"), sem("dve_steps")
        block = ctx.enter_context(nc.Block())

        @block.sync
        def _(sp):
            with sp.Fori(0, TILES1) as i:
                sp.wait_ge(s_gu, i * 2 + 1)
                sp.dma_start(wgu[:].rearrange("p k g n -> p (k g n)"), gu1[bass.ds(i, 1)].rearrange("i p n -> (i p) n")).then_inc(s_wgu, 16)
                sp.wait_ge(s_dn, i * 4 + 1)
                sp.dma_start(wd[:], down1[bass.ds(i, 1)].rearrange("i p n -> (i p) n")).then_inc(s_wd, 16)

        @block.tensor
        def _(pe):
            pe.sem_inc(s_gu, 1)
            pe.sem_inc(s_dn, 1)
            with pe.Fori(0, TILES1) as i:
                pe.wait_ge(s_wgu, i * 16 + 16)
                for half in range(2):
                    cols = slice(half * HALF, (half + 1) * HALF)
                    pe.wait_ge(s_hu, i * 2 + half + 1)
                    for which in range(2):
                        for k in range(KT):
                            mm = pe.matmul(ps[:, 2 * half + which, :], wgu[:, k, which, :], m.xnT[:, k, cols],
                                           start=k == 0, stop=k == KT - 1)
                    mm.then_inc(s_gu, 1)
                    pe.wait_ge(s_h, i * 2 + half + 1)
                    pe.matmul(ps[:, 4 + 3 * half, :], m.sel1[0:3 * ESEL, bass.ds(i * P, P)], m.wT3[0:3 * ESEL, cols],
                              start=True, stop=True).then_inc(s_w, 1)
                pe.wait_ge(s_wd, i * 16 + 16)
                for c2 in range(NC // 2):
                    if c2 % 2 == 0:
                        pe.wait_ge(s_h, i * 2 + c2 // 2 + 3)
                    pe.wait_ge(s_y, i * 4 + c2 + 1)
                    for c in (2 * c2, 2 * c2 + 1):
                        mm = pe.matmul(ps[:, 5 + c2 % 2, (c % 2) * D:(c % 2 + 1) * D], hid[:, c * P:(c + 1) * P], wd[:],
                                       start=True, stop=True)
                    mm.then_inc(s_dn, 1)

        @block.scalar
        def _(act):
            with act.Fori(0, TILES1) as i:
                for half in range(2):
                    act.wait_ge(s_gu, i * 2 + half + 2)
                    act.wait_ge(s_gs, i * 2 + half + 1)
                    nc.scalar.activation(th[:, half, :], ps[:, 2 * half, :], ACT.Tanh, scale=0.5).then_inc(s_th, 1)

        @block.vector
        def _(dve):
            step = Chain(dve, s_dve)
            step.link(dve.memset(m.yacc[:], 0.0))
            dve.sem_inc(s_hu, 2)
            dve.sem_inc(s_gs, 2)
            dve.sem_inc(s_h, 2)
            dve.sem_inc(s_y, 2)
            with dve.Fori(0, TILES1) as i:
                for half in range(2):
                    cols = slice(half * HALF, (half + 1) * HALF)
                    dve.wait_ge(s_th, i * 2 + half + 1)
                    dve.scalar_tensor_tensor(out=gs[:, half, :], in0=th[:, half, :], scalar=1.0, in1=ps[:, 2 * half, :],
                                             op0=ALU.add, op1=ALU.mult).then_inc(s_gs, 1)
                    dve.wait_ge(s_gs, i * 2 + half + 3)
                    dve.wait_ge(s_dn, i * 4 + 1)
                    dve.scalar_tensor_tensor(out=hid[:, cols], in0=gs[:, half, :], scalar=0.5, in1=ps[:, 2 * half + 1, :],
                                             op0=ALU.mult, op1=ALU.mult).then_inc(s_hu, 1)
                    dve.wait_ge(s_hu, i * 2 + half + 3)
                    dve.wait_ge(s_w, i * 2 + half + 1)
                    dve.tensor_tensor(hid[:, cols], hid[:, cols], ps[:, 4 + 3 * half, :], ALU.mult).then_inc(s_h, 1)
                for c2 in range(NC // 2):
                    dve.wait_ge(s_dn, i * 4 + c2 + 2)
                    dve.tensor_tensor(m.yacc[:, 2 * c2:2 * c2 + 2, :], m.yacc[:, 2 * c2:2 * c2 + 2, :],
                                      ps[:, 5 + c2 % 2, :].rearrange("p (c d) -> p c d", c=2), ALU.add).then_inc(s_y, 1)


BLK = 16
NB = P // BLK
FIRST = 4
DOUBLINGS = [(lv, e) for lv in range(FIRST, LEVELS) for e in range(2)]
ND = len(DOUBLINGS)
SUBS = 2 * BLK - 1
SUB_BANKS = [(0, (0, 1)), (1, (2, 3)), (2, (4, 5, 6)), (3, (7, 8, 9, 10, 11)), (4, (12, 13, 14))]


def stage_delta(nc, m, w_conv, w_z, w_out):
    with ExitStack() as ctx:
        def sb(name, shape, dt=F32):
            return ctx.enter_context(nc.sbuf_tensor(name, shape, dt))

        def sem(name):
            return ctx.enter_context(nc.semaphore(name))

        ps = m.ps
        wc = sb("w_conv_st", [P, KT, 4 * P])
        wz = sb("w_z_st", [P, KT, 2 * P])
        wo = sb("w_out_st", [P, 2, D])
        tap = sb("tap_st", [P, 4, TAPS])
        raw = sb("raw", [P, 4, TAPS - 1 + T])
        cv = sb("conv", [P, 4, T])
        thc = sb("tanh_conv", [P, T])
        kq = sb("kq", [P, NC, 2, P])
        sq = sb("squares", [P, 2, T])
        ss = sb("sumsq", [P, 2, NC])
        rn = sb("rsqrt_next", [P, 2, NC])
        rs = sb("rsqrt", [P, 2, NC])
        irk = sb("norm_k", [P, NC])
        NAMES = {n: i for i, n in enumerate(("a1", "a1_after", "egc_rq", "neg_egc", "etot"))}
        scal = sb("unit_scalars", [P, len(NAMES), 2, NC])
        knat = sb("k_nat", [P, NC, P])
        vnat = sb("v_nat", [P, 2, NC, P])
        gm_q = sb("gmask_Q", [P, 2, NC, P])
        e_p = sb("decay_P", [P, 2, NC, P])
        att = sb("att", [P, 2, NC, P])
        u = sb("U", [P, 2, NC, P])
        u32 = sb("U32", [P, UNITS, 2, BLK])
        uc = sb("U16", [P, UNITS, BLK])
        pc = sb("P16", [P, UNITS, BLK])
        pt = sb("P16_term", [P, UNITS * BLK])
        eye = sb("eye16", [P, NB, BLK])
        eye1 = sb("eye16_own", [P, BLK])
        bmask = sb("block_mask", [P, NB])
        hmask = sb("half_mask", [P, 2])
        row = sb("row_of_block", [P, BLK, P])
        xs = sb("X", [P, 2, NC, P // 2])
        st = sb("S", [P, 2, P])
        wsb = sb("W", [P, 2, 2, P])
        qs = sb("QS", [P, 2, 2, P])
        tz = sb("tanh_z", [P, 2 * P])
        zs = sb("silu_z", [P, NC, 2 * P])
        o = sb("o", [P, NC, 2, P])
        og = sb("o_gated", [P, NC, 2, P])
        osq = sb("o_squares", [P, P])
        var = sb("o_var", [P, NC, 2])
        ro = sb("o_rsqrt", [P, NC, 2])
        oT = m.xn[:].rearrange("p c d -> p (c d)").rearrange("p (e t) -> p e t", e=2)
        y = sb("y_delta", [P, NC, D])

        s_wc, s_wz, s_wo = sem("w_conv_in"), sem("w_z_in"), sem("w_out_in")
        s_pj, s_raw, s_conv, s_tc, s_cvd = (sem("projected"), sem("raw_copied"), sem("convolved"), sem("conv_tanh"),
                                            sem("conv_done"))
        s_taps, s_dconv, s_rn, s_irk = sem("taps_staged"), sem("tap_added"), sem("rsqrts_made"), sem("norms_made")
        s_sq, s_ss, s_sse, s_sc = sem("squared"), sem("sumsq_made"), sem("sumsq_eps"), sem("scalars_made")
        s_gm, s_kq, s_d, s_e, s_kk, s_u = (sem("gmask_made"), sem("kq_copied"), sem("D_made"), sem("E_made"), sem("kk_made"),
                                           sem("U_made"))
        s_u32, s_um, s_uc, s_rk, s_ch = sem("U32_copied"), sem("U32_masked"), sem("U16_made"), sem("rows_spread"), sem("chain")
        s_p0, s_p1 = sem("P_spread_0"), sem("P_spread_1")
        s_kt, s_kn, s_vn, s_qt, s_q = (sem("kv_transposed"), sem("k_nat_made"), sem("v_nat_made"), sem("P_transposed"),
                                       sem("Q_begun"))
        s_x, s_xt, s_y, s_yt, s_t, s_pt = (sem("X_made"), sem("X_taken"), sem("QX_made"), sem("QX_taken"), sem("Q_transposed"),
                                           sem("P_made"))
        s_ot, s_ote, s_op, s_ya = sem("o_transposed"), sem("oT_made"), sem("out_made"), sem("y_added")
        s_ks, s_qsm, s_r, s_w, s_wa, s_ws = (sem("KS_made"), sem("QS_made"), sem("R_made"), sem("W_made"), sem("Wa_made"),
                                             sem("Ws_made"))
        s_su, s_S, s_aw, s_qe, s_o = sem("S_update"), sem("S_made"), sem("AW_made"), sem("QS_scaled"), sem("O_made")
        s_zp, s_tz, s_zs, s_oz, s_var, s_rr, s_og = (sem("z_made"), sem("z_tanh"), sem("z_silu"), sem("oz_made"),
                                                     sem("o_var_made"), sem("o_rsqrt_made"), sem("og_made"))
        s_dve, s_pool, s_init, s_passed = sem("dve_steps"), sem("pool_steps"), sem("constants_made"), sem("pool_wait_passed")
        block = ctx.enter_context(nc.Block())

        def sc(name, e, c):
            return scal[:, NAMES[name], e, c:c + 1]

        def chunks(ap):
            return ap.rearrange("p c i -> p (c i)")

        KS_BANK, W_BANK = (0, 2), (1, 7)

        def two_banks(b):
            return ps[:, b:b + 2, :].rearrange("p b n -> p (b n)")

        def sub_columns(k):
            for bank, ks in SUB_BANKS:
                at = 0
                for q in ks:
                    if q == k:
                        return bank, at
                    at += UNITS * (BLK - 1 - q)

        @block.sync
        def _(sp):
            sp.dma_start(wc[:].rearrange("p k n -> p (k n)"), w_conv[0]).then_inc(s_wc, 16)
            sp.dma_start(wo[:].rearrange("p e n -> p (e n)"), w_out[0]).then_inc(s_wo, 16)
            with sp.Fori(0, NK) as i:
                sp.wait_ge(s_pj, i * 8 + 8)
                sp.dma_start(wc[:].rearrange("p k n -> p (k n)"), w_conv[bass.ds(i + 1, 1)].rearrange("i p n -> (i p) n")).then_inc(s_wc, 16)
                sp.wait_ge(s_zp, i * NC + 1)
                sp.dma_start(wz[:].rearrange("p k n -> p (k n)"), w_z[bass.ds(i, 1)].rearrange("i p n -> (i p) n")).then_inc(s_wz, 16)
                sp.wait_ge(s_op, i * 4 + 4)
                sp.dma_start(wo[:].rearrange("p e n -> p (e n)"), w_out[bass.ds(i, 1)].rearrange("i p n -> (i p) n")).then_inc(s_wo, 16)

        @block.tensor
        def _(pe):
            pe.sem_inc(s_zp, 1)

            def project(r, n):
                if n == 0:
                    pe.wait_ge(s_wc, r * 16 + 16)
                if n > 1:
                    pe.wait_ge(s_raw, r * 8 + n - 1)
                for k in range(KT):
                    mm = pe.matmul(ps[:, 6 + n % 2, :], wc[:, k, (n // 2) * P:(n // 2 + 1) * P],
                                   m.xnT[:, k, (n % 2) * HALF:(n % 2 + 1) * HALF], start=k == 0, stop=k == KT - 1)
                mm.then_inc(s_pj, 1)

            def sum_squares(r):
                pe.wait_ge(s_sq, r * 2 + 2)
                pe.wait_ge(s_raw, r * 8 + 7)
                for n in range(2):
                    for c in range(NC):
                        mm = pe.matmul(ps[:, 6, n * NC + c:n * NC + c + 1], sq[:, n, c * P:(c + 1) * P], m.ones[:, 0:1],
                                       start=True, stop=True)
                mm.then_inc(s_ss, 1)

            def turn_outputs(i, n):
                e, half = n // 2, n % 2
                if n == 0:
                    pe.wait_ge(s_og, i + 1)
                for c in range(4):
                    mm = pe.transpose(ps[:, n, c * P:(c + 1) * P], og[:, 4 * half + c, e, :], m.ident[:])
                mm.then_inc(s_ot, 1)

            def project_out(i, n):
                if n == 0:
                    pe.wait_ge(s_wo, i * 16 + 16)
                    pe.wait_ge(s_ote, i * 4 + 4)
                if n >= 2:
                    pe.wait_ge(s_ya, i * 4 + n)
                for c in (2 * n, 2 * n + 1):
                    for e in range(2):
                        mm = pe.matmul(ps[:, n % 2, (c % 2) * D:(c % 2 + 1) * D], oT[:, e, c * P:(c + 1) * P], wo[:, e, :],
                                       start=e == 0, stop=e == 1)
                mm.then_inc(s_op, 1)

            def project_z(i, c, bank):
                if c == 0:
                    pe.wait_ge(s_wz, i * 16 + 16)
                if c >= 2 and c != 4:
                    pe.wait_ge(s_zs, i * NC + (c if c < 4 else c + 1))
                for k in range(KT):
                    mm = pe.matmul(ps[:, bank, 0:256], m.xnT[:, k, c * P:(c + 1) * P], wz[:, k, :], start=k == 0, stop=k == KT - 1)
                mm.then_inc(s_zp, 1)

            for n in range(8):
                project(0, n)
            sum_squares(0)
            pe.wait_ge(s_init, 7 + NB)
            with pe.Fori(0, NK) as i:
                pe.wait_ge(s_gm, i + 1)
                for b in range(4):
                    if b == 3:
                        pe.wait_ge(s_o, i * NC + 1)
                    pe.matmul(ps[:, b, :], m.after[:], chunks(gm_q[:, b // 2, 4 * (b % 2):4 * (b % 2) + 4, :]),
                              start=True, stop=False)
                    mm = pe.matmul(ps[:, b, :], m.identb[:], m.future[:].unsqueeze(1).broadcast_to([P, 4, P]),
                                   start=False, stop=True)
                    mm.then_inc(s_d, 1)
                pe.wait_ge(s_kq, i + 1)
                pe.wait_ge(s_zs, i * NC + 1)
                pe.wait_ge(s_sse, i + 1)
                pe.wait_ge(s_raw, i * 8 + 8)
                for b in range(4):
                    for c in (2 * b, 2 * b + 1):
                        mm = pe.matmul(ps[:, 4 + b, (c % 2) * 256:(c % 2 + 1) * 256], kq[:, c, 0, :],
                                       kq[:, c, :, :].rearrange("p a i -> p (a i)"), start=True, stop=True)
                    mm.then_inc(s_kk, 1)
                pe.wait_ge(s_e, i * 4 + 4)

                def turn_kv(n, bank):
                    for c in range(NC):
                        mm = pe.transpose(ps[:, bank + c // 4, (c % 4) * P:(c % 4 + 1) * P], cv[:, n, c * P:(c + 1) * P], m.ident[:])
                    mm.then_inc(s_kt, 1)

                project_z(i, 0, 2)
                project_z(i, 1, 3)
                pe.wait_ge(s_cvd, i * 4 + 4)
                pe.wait_ge(s_u, i * 4 + 2)
                turn_kv(1, 4)
                pe.wait_ge(s_u, i * 4 + 4)
                turn_kv(2, 6)
                for n in range(4):
                    if n == 2:
                        pe.wait_ge(s_zs, i * NC + 3)
                    turn_outputs(i, n)
                pe.wait_ge(s_kn, i + 1)
                turn_kv(3, 4)
                for n in range(4):
                    project_out(i, n)
                    if n < 2:
                        project_z(i, 2 + n, 2 + n)
                pe.wait_ge(s_uc, i + 1)
                pe.wait_ge(s_ya, i * 4 + 5)
                pe.wait_ge(s_zs, i * NC + 5)
                pe.wait_ge(s_vn, i * 2 + 2)
                for bank, ks in SUB_BANKS:
                    for k in ks:
                        at, n = sub_columns(k)[1], BLK - 1 - k
                        mm = pe.matmul(ps[:, bank, at:at + UNITS * n], row[:, k, :], uc[:, :, k + 1:], start=True, stop=True)
                    mm.then_inc(s_rk, 1)
                for n in range(4):
                    project(i + 1, n)
                for e in range(2):
                    pe.wait_ge(s_p0 if e == 0 else s_p1, i + 1)
                    for c in range(NC):
                        mm = pe.transpose(ps[:, 2 * e + c // 4, (c % 4) * P:(c % 4 + 1) * P], e_p[:, e, c, :], m.ident[:])
                    mm.then_inc(s_qt, 1)
                pe.wait_ge(s_q, i * 2 + 2)
                for lv in range(FIRST, LEVELS):
                    s = 1 << lv
                    n0 = 2 * (lv - FIRST)
                    for e in range(2):
                        if lv > FIRST:
                            pe.wait_ge(s_yt, i * ND + n0 + e - 1)
                        for c in range(NC):
                            dst = ps[:, e, c * 64:(c + 1) * 64].rearrange("p (b s) -> p b s", s=s)
                            mm = pe.matmul(dst, u[:, e, c, :], gm_q[:, e, c, :].rearrange("p (b t s) -> p b t s", t=2, s=s)[:, :, 0, :],
                                           start=True, stop=True)
                        mm.then_inc(s_x, 1)
                    for e in range(2):
                        pe.wait_ge(s_xt, i * ND + n0 + e + 1)
                        if lv > FIRST:
                            pe.wait_ge(s_pt, i * ND + n0 + e - 1)
                        for c in range(NC):
                            mm = pe.matmul(ps[:, e, c * 64:(c + 1) * 64], e_p[:, e, c, :], xs[:, e, c, :], start=True, stop=True)
                        mm.then_inc(s_y, 1)
                    if lv < LEVELS - 1:
                        project(i + 1, 2 * (lv - FIRST) + 4)
                    else:
                        sum_squares(i + 1)
                    for e in range(2):
                        pe.wait_ge(s_yt, i * ND + n0 + e + 1)
                        for c in range(NC):
                            mm = pe.transpose(ps[:, 2 + 2 * e + c // 4, (c % 4) * P:(c % 4 + 1) * P], gm_q[:, e, c, :], m.ident[:])
                        mm.then_inc(s_t, 1)
                    if lv < LEVELS - 1:
                        project(i + 1, 2 * (lv - FIRST) + 5)
                pe.wait_ge(s_pt, i * ND + ND)
                for c in range(NC):
                    if c:
                        for e in range(2):
                            pe.wait_ge(s_S, i * 14 + 2 * c + e - 1)
                            pe.matmul(ps[:, KS_BANK[e], 0:P], kq[:, c, 0, :], st[:, e, :], start=True, stop=True).then_inc(s_ks, 1)
                        if c > 1:
                            pe.wait_ge(s_qe, i * 7 + c - 1)
                        pe.matmul(ps[:, 4, 0:256], kq[:, c, 1, :], st[:].rearrange("p e n -> p (e n)"),
                                  start=True, stop=True).then_inc(s_qsm, 1)
                    if c >= 4:
                        project_z(i, c, 5)
                    if c:
                        pe.wait_ge(s_wa, i * NC + c)
                    else:
                        pe.wait_ge(s_raw, i * 8 + 16)
                    for e in range(2):
                        if c:
                            pe.wait_ge(s_r, i * 14 + 2 * c + e - 1)
                        pe.matmul(ps[:, W_BANK[e], 0:P], e_p[:, e, c, :], vnat[:, e, c, :], start=True, stop=True).then_inc(s_w, 1)
                    if c < NC - 1:
                        for e in range(2):
                            pe.wait_ge(s_ws, i * 14 + 2 * c + e + 1)
                            pe.matmul(ps[:, KS_BANK[e], 0:P], knat[:, c, :], wsb[:, 1, e, :], start=True, stop=True).then_inc(s_su, 1)
                    if c:
                        pe.wait_ge(s_o, i * NC + c + 1)
                    pe.wait_ge(s_wa, i * NC + c + 1)
                    for e in range(2):
                        mm = pe.matmul(ps[:, 3, e * P:(e + 1) * P], att[:, e, c, :], wsb[:, 0, e, :], start=True, stop=True)
                    mm.then_inc(s_aw, 1)
            pe.wait_ge(s_o, NK * NC + 1)
            for n in range(4):
                turn_outputs(NK, n)
            for n in range(4):
                project_out(NK, n)

        @block.scalar
        def _(act):
            def copy_raw(r, n):
                act.wait_ge(s_pj, r * 8 + n + 1)
                if isinstance(r, int):
                    if n == 0:
                        act.wait_ge(s_init, 1)
                else:
                    act.wait_ge(s_conv, r * 4 + (n // 2) - 3)
                at = TAPS - 1 + (n % 2) * HALF
                nc.scalar.copy(raw[:, n // 2, at:at + HALF], ps[:, 6 + n % 2, :]).then_inc(s_raw, 1)

            def tanh_conv(r, t):
                act.wait_ge(s_conv, r * 4 + t + 1)
                if not (isinstance(r, int) and t == 0):
                    act.wait_ge(s_cvd, r * 4 + t)
                nc.scalar.activation(thc[:], cv[:, t, :], ACT.Tanh).then_inc(s_tc, 1)

            def squares(r):
                act.wait_ge(s_cvd, r * 4 + 2)
                for n in range(2):
                    nc.scalar.activation(sq[:, n, :], cv[:, n, :], ACT.Square).then_inc(s_sq, 1)

            def copy_kq(r):
                act.wait_ge(s_cvd, r * 4 + 2)
                for n in range(2):
                    op = nc.scalar.copy(kq[:, :, n, :], cv[:, 1 - n, :].rearrange("p (c i) -> p c i", i=P))
                op.then_inc(s_kq, 1)

            def variance(i, c):
                act.wait_ge(s_o, i * NC + c + 2)
                for e in range(2):
                    nc.scalar.activation(osq[:], o[:, c, e, :], ACT.Square, accum_out=var[:, c, e:e + 1]).then_inc(s_var, 1)
                    act.wait_ge(s_var, i * 16 + 2 * c + e + 1)

            def turn_out(i, n):
                act.wait_ge(s_ot, i * 4 + n + 1)
                e, half = n // 2, n % 2
                nc.scalar.activation(oT[:, e, half * HALF:(half + 1) * HALF], ps[:, n, :], ACT.Copy,
                                     scale=m.norm_w[:, 0:1]).then_inc(s_ote, 1)

            def tanh_z(i, c):
                act.wait_ge(s_zp, i * NC + c + 2)
                act.wait_ge(s_zs, i * NC + c + 1)
                nc.scalar.activation(tz[:], ps[:, 2 + c % 2 if c < 4 else 5, 0:256], ACT.Tanh, scale=0.5).then_inc(s_tz, 1)

            for n in range(8):
                copy_raw(0, n)
            for t in range(4):
                tanh_conv(0, t)
                if t == 1:
                    squares(0)
            copy_kq(0)
            with act.Fori(0, NK) as i:
                for b in range(4):
                    act.wait_ge(s_d, i * 4 + b + 1)
                    nc.scalar.activation(chunks(e_p[:, b // 2, 4 * (b % 2):4 * (b % 2) + 4, :]), ps[:, b, :], ACT.Exp).then_inc(s_e, 1)
                tanh_z(i, 0)
                act.wait_ge(s_kt, i * 3 + 1)
                nc.scalar.copy(chunks(knat[:]), two_banks(4)).then_inc(s_kn, 1)
                tanh_z(i, 1)
                act.wait_ge(s_u, i * 4 + 4)
                uu = u[:].rearrange("p e c i -> p (e c) i")
                for q in range(4):
                    rows = slice(32 * q, 32 * q + 32)
                    nc.scalar.copy(u32[rows].rearrange("p u t i -> p u (t i)"), uu[rows, :, rows]).then_inc(s_u32, 1)
                for n in range(4):
                    turn_out(i, n)
                for c in range(2, 4):
                    tanh_z(i, c)
                for n in range(4):
                    copy_raw(i + 1, n)
                for e in range(2):
                    act.wait_ge(s_qt, i * 2 + e + 1)
                    nc.scalar.copy(chunks(gm_q[:, e]), two_banks(2 * e)).then_inc(s_q, 1)
                tanh_conv(i + 1, 0)
                for n, (lv, e) in enumerate(DOUBLINGS):
                    if e == 0:
                        if lv == FIRST + 1:
                            tanh_conv(i + 1, 1)
                        if lv < LEVELS - 1:
                            copy_raw(i + 1, 2 * (lv - FIRST) + 4)
                        else:
                            squares(i + 1)
                    act.wait_ge(s_t, i * ND + n + 1)
                    nc.scalar.copy(chunks(e_p[:, e]), two_banks(2 + 2 * e)).then_inc(s_pt, 1)
                    if e == 1 and lv < LEVELS - 1:
                        copy_raw(i + 1, 2 * (lv - FIRST) + 5)
                tanh_conv(i + 1, 2)
                for c in range(NC):
                    if c:
                        act.wait_ge(s_qsm, i * 7 + c)
                        act.wait_ge(s_o, i * NC + c)
                        for e in range(2):
                            op = nc.scalar.activation(qs[:, c % 2, e, :], ps[:, 4, e * P:(e + 1) * P], ACT.Copy,
                                                      scale=sc("egc_rq", e, c))
                        op.then_inc(s_qe, 1)
                    for e in range(2):
                        act.wait_ge(s_w, i * 16 + 2 * c + e + 1)
                        if c < NC - 1:
                            act.wait_ge(s_ws, i * 14 + 2 * c + e + 1)
                        op = nc.scalar.activation(wsb[:, 0, e, :], ps[:, W_BANK[e], 0:P], ACT.Copy, scale=sc("a1", e, c))
                    op.then_inc(s_wa, 1)
                    if c >= 4:
                        tanh_z(i, c)
                    if c:
                        variance(i, c - 1)
                    if c == 2:
                        tanh_conv(i + 1, 3)
                    if c == NC - 1:
                        copy_kq(i + 1)
                variance(i, NC - 1)
            for n in range(4):
                turn_out(NK, n)
            nc.scalar.activation(zs[:], m.yacc[:], ACT.Tanh, scale=0.5).then_inc(s_tz, 1)

        @block.gpsimd
        def _(pool):
            g = nc.gpsimd

            def passed():
                pool.sem_inc(s_passed, 1)

            def gmask(r):
                gsrc = m.g[:, 0:2, :] if isinstance(r, int) else m.g[:, bass.ds(2 * r, 2), :]
                g.tensor_tensor(gm_q[:], m.upto[:].unsqueeze(1).unsqueeze(1).broadcast_to([P, 2, NC, P]),
                                gsrc.unsqueeze(3).broadcast_to([P, 2, NC, P]), ALU.mult).then_inc(s_gm, 1)

            def rsqrts(r):
                pool.wait_ge(s_sse, r + 1)
                g.tensor_tensor(rn[:], ss[:], m.minus_half[:, 0:1].unsqueeze(2).broadcast_to([P, 2, NC]), ALU.pow).then_inc(s_rn, 1)
                g.tensor_tensor(irk[:], ss[:, 1, :], m.plus_half[:, 0:1].broadcast_to([P, NC]), ALU.pow).then_inc(s_irk, 1)

            def scalars(r):
                step = Chain(pool, s_pool, r * 2)
                heads = slice(0, 2) if isinstance(r, int) else bass.ds(2 * r, 2)
                both = [P, 2, NC]
                pool.wait_ge(s_rn, r + 1)
                passed()
                step(g.tensor_scalar(rs[:, 0, :], rn[:, 0, :], float(DK) ** -0.5, None, ALU.mult))
                step.link(g.tensor_tensor(rs[:, 1, :], rn[:, 1, :], rn[:, 1, :], ALU.mult))
                rk2 = rs[:, 1, :].unsqueeze(1).broadcast_to(both)
                rq = rs[:, 0, :].unsqueeze(1).broadcast_to(both)
                g.tensor_tensor(scal[:, NAMES["a1"]], m.beta[:, heads, :], rk2, ALU.mult).then_inc(s_sc, 1)
                pool.wait_ge(s_sc, r * 5 + 1)
                g.tensor_tensor(scal[:, NAMES["a1_after"]], m.eg[:, 1, heads, :], scal[:, NAMES["a1"]], ALU.mult).then_inc(s_sc, 1)
                g.tensor_tensor(scal[:, NAMES["egc_rq"]], m.eg[:, 0, heads, :], rq, ALU.mult).then_inc(s_sc, 1)
                g.tensor_copy(scal[:, NAMES["neg_egc"]], m.neg_egc[:, heads, :]).then_inc(s_sc, 1)
                g.tensor_copy(scal[:, NAMES["etot"]], m.eg[:, 2, heads, :]).then_inc(s_sc, 1)

            def fix(ap, op, base, pattern, cm, fill):
                fix.n += 1
                g.affine_select(out=ap, in_=ap, compare_op=op, fill=fill, base=base, pattern=pattern,
                                channel_multiplier=cm).then_inc(s_init, 1)
                pool.wait_ge(s_init, fix.n)
            g.memset(raw[:, :, 0:TAPS - 1], 0.0).then_inc(s_init, 1)
            g.tensor_copy(tap[:], m.taps[:, 0]).then_inc(s_taps, 1)
            g.memset(eye[:], 0.0).then_inc(s_init, 1)
            g.memset(bmask[:], 1.0).then_inc(s_init, 1)
            g.memset(row[:], 0.0).then_inc(s_init, 1)
            pool.wait_ge(s_init, 4)
            fix.n = 4
            fix(eye[:], ALU.not_equal, 0, [[-BLK, NB], [-1, BLK]], 1, 1.0)
            fix(bmask[:], ALU.is_ge, 0, [[-BLK, NB]], 1, 0.0)
            fix(bmask[:], ALU.is_ge, BLK - 1, [[BLK, NB]], -1, 0.0)
            assert fix.n == 7
            gmask(0)
            for b in range(NB):
                ap = row[:, :, b * BLK:(b + 1) * BLK]
                g.affine_select(out=ap, in_=ap, compare_op=ALU.not_equal, fill=1.0, base=-BLK * b,
                                pattern=[[-1, BLK], [0, BLK]], channel_multiplier=1).then_inc(s_init, 1)
            rsqrts(0)
            scalars(0)
            pool.wait_ge(s_cvd, 4)
            passed()
            g.tensor_copy(tap[:], m.taps[:, 1]).then_inc(s_taps, 1)
            with pool.Fori(0, NK) as i:
                pool.wait_ge(s_ch, i * SUBS + SUBS)
                pool.wait_ge(s_u, i * 4 + 4)
                g.tensor_tensor(e_p[:, 1].rearrange("p c (b i) -> p c b i", i=BLK),
                                pc[:, NC:, :].unsqueeze(2).broadcast_to([P, NC, NB, BLK]),
                                bmask[:].unsqueeze(1).unsqueeze(3).broadcast_to([P, NC, NB, BLK]), ALU.mult).then_inc(s_p1, 1)
                pool.wait_ge(s_t, i * ND + ND)
                gmask(i + 1)
                pool.wait_ge(s_ot, i * 4 + 4)
                for c in range(NC):
                    if c == 2:
                        rsqrts(i + 1)
                    pool.wait_ge(s_o, i * NC + c + 2)
                    if c == NC - 1:
                        scalars(i + 1)
                    pool.wait_ge(s_zs, i * NC + c + 2)
                    g.tensor_tensor(og[:, c].rearrange("p e n -> p (e n)"), o[:, c].rearrange("p e n -> p (e n)"), zs[:, c, :],
                                    ALU.mult).then_inc(s_oz, 1)
                pool.wait_ge(s_var, i * 16 + 16)
                passed()
                g.tensor_scalar(ro[:], var[:], 1.0 / DK, 1e-6, ALU.mult, ALU.add).then_inc(s_rr, 1)
                pool.wait_ge(s_rr, i * 2 + 3)
                g.tensor_tensor(ro[:], ro[:], m.minus_half[:, 0:1].unsqueeze(2).broadcast_to([P, NC, 2]), ALU.pow).then_inc(s_rr, 1)
                pool.wait_ge(s_cvd, i * 4 + 8)
                passed()
                g.tensor_copy(tap[:], m.taps[:, bass.ds(i + 2, 1), :, :].rearrange("p a b c -> p (a b) c")).then_inc(s_taps, 1)

        @block.vector
        def _(dve):
            step = Chain(dve, s_dve)

            def conv_op(r, t, k):
                if k == 0:
                    dve.wait_ge(s_raw, r * 8 + 2 * t + 2)
                    dve.wait_ge(s_taps, r + 1)
                at = TAPS - 1 - k
                if k == 0:
                    op = dve.tensor_scalar(cv[:, t, :], raw[:, t, at:at + T], tap[:, t, TAPS - 1:TAPS], None, ALU.mult)
                elif k < TAPS:
                    op = dve.scalar_tensor_tensor(out=cv[:, t, :], in0=raw[:, t, at:at + T], scalar=tap[:, t, at:at + 1],
                                                  in1=cv[:, t, :], op0=ALU.mult, op1=ALU.add)
                if k < TAPS - 1:
                    op.then_inc(s_dconv, 1)
                    dve.wait_ge(s_dconv, r * 12 + t * 3 + k + 1)
                elif k == TAPS - 1:
                    op.then_inc(s_conv, 1)
                else:
                    dve.wait_ge(s_tc, r * 4 + t + 1)
                    dve.scalar_tensor_tensor(out=cv[:, t, :], in0=thc[:], scalar=1.0, in1=cv[:, t, :],
                                             op0=ALU.add, op1=ALU.mult).then_inc(s_cvd, 1)

            def add_eps(r):
                dve.wait_ge(s_ss, r + 1)
                dve.tensor_scalar(ss[:].rearrange("p n c -> p (n c)"), ps[:, 6, 0:2 * NC], 1e-6, None, ALU.add).then_inc(s_sse, 1)

            def add_out(i, n):
                dve.wait_ge(s_op, i * 4 + n + 1)
                dve.tensor_tensor(y[:, 2 * n:2 * n + 2, :], y[:, 2 * n:2 * n + 2, :],
                                  ps[:, n % 2, :].rearrange("p (c d) -> p c d", c=2), ALU.add).then_inc(s_ya, 1)

            def silu_z(i, c):
                dve.wait_ge(s_tz, i * NC + c + 1)
                dve.wait_ge(s_oz, i * NC + c + 1)
                dve.scalar_tensor_tensor(out=zs[:, c, :], in0=tz[:], scalar=1.0, in1=ps[:, 2 + c % 2 if c < 4 else 5, 0:256],
                                         op0=ALU.add, op1=ALU.mult).then_inc(s_zs, 1)

            step.link(dve.memset(y[:], 0.0))
            dve.sem_inc(s_o, 1)
            dve.sem_inc(s_zs, 1)
            dve.sem_inc(s_ya, 1)
            dve.sem_inc(s_rr, 2)
            dve.sem_inc(s_oz, NC)
            dve.memset(og[:], 0.0).then_inc(s_dve, 1)
            dve.memset(ro[:], 0.0).then_inc(s_dve, 1)
            dve.wait_ge(s_dve, 3)
            step.n = 3
            dve.wait_ge(s_init, 7)
            step.link(dve.tensor_reduce(eye1[:], eye[:].rearrange("p b i -> p i b"), AX.X, ALU.add))
            step.link(dve.tensor_reduce(hmask[:], bmask[:].rearrange("p (q t) -> p t q", t=2), AX.X, ALU.add))
            for t in range(4):
                for k in range(TAPS + 1):
                    conv_op(0, t, k)
                if t == 2:
                    add_eps(0)
            with dve.Fori(0, NK) as i:
                dve.wait_ge(s_sc, i * 5 + 5)
                dve.wait_ge(s_e, i * 4 + 4)
                for b in range(4):
                    dve.wait_ge(s_kk, i * 4 + b + 1)
                    kk = ps[:, 4 + b, :].rearrange("p (c a n) -> p c a n", c=2, a=2)
                    for e in range(2):
                        dve.tensor_tensor(att[:, e, 2 * b:2 * b + 2, :], kk[:, :, 1, :], e_p[:, e, 2 * b:2 * b + 2, :], ALU.mult)
                        for c in (2 * b, 2 * b + 1):
                            op = dve.scalar_tensor_tensor(out=u[:, e, c, :], in0=kk[:, c % 2, 0, :], scalar=sc("a1", e, c),
                                                          in1=e_p[:, e, c, :], op0=ALU.mult, op1=ALU.mult)
                    op.then_inc(s_u, 1)
                    if b % 2:
                        silu_z(i, b // 2)
                dve.wait_ge(s_rr, i * 2 + 2)
                dve.wait_ge(s_oz, i * NC + NC)
                dve.tensor_tensor(og[:], og[:], ro[:].unsqueeze(3).broadcast_to([P, NC, 2, P]), ALU.mult).then_inc(s_og, 1)
                dve.wait_ge(s_u32, i * 4 + 4)
                dve.tensor_tensor(u32[:], u32[:], hmask[:].unsqueeze(1).unsqueeze(3).broadcast_to([P, UNITS, 2, BLK]),
                                  ALU.mult).then_inc(s_um, 1)
                dve.wait_ge(s_um, i + 1)
                dve.tensor_tensor(uc[:], u32[:, :, 0, :], u32[:, :, 1, :], ALU.add).then_inc(s_uc, 1)
                dve.wait_ge(s_irk, i + 1)
                for e in range(2):
                    dve.wait_ge(s_kt, i * 3 + e + 2)
                    dve.tensor_tensor(vnat[:, e], ps[:, (6, 4)[e]:(6, 4)[e] + 2, :].rearrange("p b (c n) -> p (b c) n", n=P),
                                      irk[:].unsqueeze(2).broadcast_to([P, NC, P]), ALU.mult).then_inc(s_vn, 1)
                for n in range(4):
                    add_out(i, n)
                    if n < 2:
                        silu_z(i, 2 + n)
                n = 1
                dve.tensor_copy(pc[:], eye1[:].unsqueeze(1).broadcast_to([P, UNITS, BLK])).then_inc(s_ch, 1)
                for b, (bank, ks) in enumerate(SUB_BANKS):
                    dve.wait_ge(s_rk, i * len(SUB_BANKS) + b + 1)
                    for k in ks:
                        at, w = sub_columns(k)[1], BLK - 1 - k
                        term = pt[:, 0:UNITS * w].rearrange("p (u i) -> p u i", i=w)
                        dve.wait_ge(s_ch, i * SUBS + n)
                        dve.tensor_tensor(term, ps[:, bank, at:at + UNITS * w].rearrange("p (u i) -> p u i", i=w),
                                          pc[:, :, k:k + 1].broadcast_to([P, UNITS, w]), ALU.mult).then_inc(s_ch, 1)
                        dve.wait_ge(s_ch, i * SUBS + n + 1)
                        dve.tensor_tensor(pc[:, :, k + 1:], pc[:, :, k + 1:], term, ALU.subtract).then_inc(s_ch, 1)
                        n += 2
                assert n == SUBS
                dve.wait_ge(s_ch, i * SUBS + n)
                dve.tensor_tensor(e_p[:, 0].rearrange("p c (b i) -> p c b i", i=BLK),
                                  pc[:, 0:NC, :].unsqueeze(2).broadcast_to([P, NC, NB, BLK]),
                                  bmask[:].unsqueeze(1).unsqueeze(3).broadcast_to([P, NC, NB, BLK]), ALU.mult).then_inc(s_p0, 1)
                todo = ([(0, k) for k in range(TAPS)] + [(1, 0), (0, TAPS)] + [(1, k) for k in range(1, TAPS)]
                        + [(1, TAPS)] + [(2, k) for k in range(TAPS)] + [(3, 0), (3, 1), (3, 2), (2, TAPS), (3, 3), (3, TAPS)])

                def more(n=1):
                    for _ in range(n):
                        if todo:
                            conv_op(i + 1, *todo.pop(0))

                dve.wait_ge(s_kq, i + 1)
                more(4)
                for lv in range(FIRST, LEVELS):
                    s, n0 = 1 << lv, 2 * (lv - FIRST)
                    for e in range(2):
                        dve.wait_ge(s_x, i * ND + n0 + e + 1)
                        mask = m.lmask[:, lv, :].unsqueeze(1).broadcast_to([P, NC, 64])
                        dve.tensor_tensor(xs[:, e], ps[:, e, :].rearrange("p (c n) -> p c n", c=NC), mask, ALU.mult).then_inc(s_xt, 1)
                        if e == 0:
                            more(1)
                    for e in range(2):
                        dve.wait_ge(s_y, i * ND + n0 + e + 1)
                        dst = gm_q[:, e, :, :].rearrange("p c (b t s) -> p c b t s", t=2, s=s)[:, :, :, 0, :]
                        dve.tensor_tensor(dst, dst, ps[:, e, :].rearrange("p (c b s) -> p c b s", c=NC, s=s), ALU.subtract).then_inc(s_yt, 1)
                    more(3)
                def outputs(c):
                    dve.wait_ge(s_aw, i * NC + c + 1)
                    if c == 0:
                        op = dve.tensor_scalar(o[:, c, :, :], ps[:, 3, 0:256].rearrange("p (e n) -> p e n", e=2),
                                               rs[:, 0, c:c + 1], None, ALU.mult)
                    else:
                        dve.wait_ge(s_qe, i * 7 + c)
                        for e in range(2):
                            op = dve.scalar_tensor_tensor(out=o[:, c, e, :], in0=ps[:, 3, e * P:(e + 1) * P],
                                                          scalar=rs[:, 0, c:c + 1], in1=qs[:, c % 2, e, :],
                                                          op0=ALU.mult, op1=ALU.add)
                    op.then_inc(s_o, 1)

                more(1)
                for c in range(NC):
                    if c:
                        for e in range(2):
                            dve.wait_ge(s_ks, i * 14 + 2 * c + e - 1)
                            dve.scalar_tensor_tensor(out=vnat[:, e, c, :], in0=ps[:, KS_BANK[e], 0:P],
                                                     scalar=sc("neg_egc", e, c), in1=vnat[:, e, c, :],
                                                     op0=ALU.mult, op1=ALU.add).then_inc(s_r, 1)
                    if c < NC - 1:
                        for e in range(2):
                            dve.wait_ge(s_w, i * 16 + 2 * c + e + 1)
                            dve.tensor_scalar(wsb[:, 1, e, :], ps[:, W_BANK[e], 0:P], sc("a1_after", e, c), None,
                                              ALU.mult).then_inc(s_ws, 1)
                    if c:
                        outputs(c - 1)
                    if c < NC - 1:
                        for e in range(2):
                            dve.wait_ge(s_su, i * 14 + 2 * c + e + 1)
                            if c == 0:
                                op = dve.tensor_copy(st[:, e, :], ps[:, KS_BANK[e], 0:P])
                            else:
                                op = dve.scalar_tensor_tensor(out=st[:, e, :], in0=st[:, e, :], scalar=sc("etot", e, c),
                                                              in1=ps[:, KS_BANK[e], 0:P], op0=ALU.mult, op1=ALU.add)
                            op.then_inc(s_S, 1)
                    if c == 1:
                        add_eps(i + 1)
                    if c in (0, 1, 3):
                        more(1)
                    if c >= 4:
                        silu_z(i, c)
                outputs(NC - 1)
                assert not todo
            dve.wait_ge(s_rr, NK * 2 + 2)
            dve.wait_ge(s_oz, NK * NC + NC)
            dve.tensor_tensor(og[:], og[:], ro[:].unsqueeze(3).broadcast_to([P, NC, 2, P]), ALU.mult).then_inc(s_og, 1)
            for n in range(4):
                add_out(NK, n)
            dve.wait_ge(s_tz, NK * NC + 1)
            dve.wait_ge(s_ya, NK * 4 + 5)
            step.link(dve.scalar_tensor_tensor(out=m.yacc[:], in0=zs[:], scalar=1.0, in1=m.yacc[:], op0=ALU.add, op1=ALU.mult))
            step.link(dve.scalar_tensor_tensor(out=m.yacc[:], in0=m.yacc[:], scalar=0.5, in1=y[:], op0=ALU.mult, op1=ALU.mult))
            step.link(dve.tensor_tensor(m.x[:], m.x[:], m.yacc[:], ALU.add))


def kernel(**inputs):
    import numpy as _np
    import concourse.bacc as _bacc
    from concourse import mybir as _mybir
    from concourse.bass_utils import run_bass_kernel_spmd as _run

    a = {k: _np.asarray(v) for k, v in inputs.items()}
    packed = {
        "x": a["L0_attn_x"],
        "w_attn": _np.concatenate([a["L0_attn_wq"], a["L0_attn_wk"], a["L0_attn_wv"]], axis=1),
        "w_o": a["L0_attn_wo"],
        "gate0": a["L0_ffn_gate"],
        "gu0": a["L0_ffn_gate_up_proj"].reshape(8, 4, 2, 128, 2, 96).transpose(0, 3, 2, 4, 1, 5).reshape(8, 128, -1),
        "down0": a["L0_ffn_down_proj"].reshape(8, 3, 128, 256).transpose(0, 2, 1, 3).reshape(8, 128, -1),
        "w_conv": _key_head_groups(_np, a["L1_attn_W_qkv"]).reshape(2, 128, 17, 512).transpose(2, 1, 0, 3).reshape(17, 128, -1),
        "w_tap": _key_head_groups(_np, a["L1_attn_conv_w"].T).reshape(4, 17, 4, 128).transpose(3, 1, 2, 0).reshape(128, -1),
        "w_z": a["L1_attn_W_z"].reshape(2, 128, 16, 256).transpose(2, 1, 0, 3).reshape(16, 128, -1),
        "w_out": a["L1_attn_W_out"].reshape(16, 2, 128, 256).transpose(0, 2, 1, 3).reshape(16, 128, -1),
        "w_ba": _np.concatenate([a["L1_attn_W_b"], a["L1_attn_W_a"]], axis=1),
        "dt_bias": a["L1_attn_dt_bias"].reshape(1, 32),
        "a_log": a["L1_attn_A_log"].reshape(1, 32),
        "norm_w": a["L1_attn_norm_w"].reshape(128, 1),
        "router1": a["L1_ffn_Wr"],
        "gu1": _np.stack([a["L1_ffn_Wg"], a["L1_ffn_Wu"]]).transpose(2, 0, 1, 3).reshape(2, 128, 2, 11, 128)
                  .transpose(3, 1, 0, 2, 4).reshape(11, 128, -1),
        "down1": a["L1_ffn_Wd"].reshape(11, 128, 256),
    }
    nc = _bacc.Bacc("TRN2", target_bir_lowering=False, num_devices=1)
    arrays, args = {}, []
    for name, v in packed.items():
        v = _np.ascontiguousarray(v)
        arrays[f"in_{name}"] = v
        args.append(nc.dram_tensor(f"in_{name}", v.shape, _mybir.dt.from_np(v.dtype), kind="ExternalInput").ap())
    args.append(nc.dram_tensor("out_0", (1, 1024, 256), _mybir.dt.float32, kind="ExternalOutput").ap())
    build(nc, *args)
    r = _run(nc, [arrays], core_ids=[0])
    return r.results[0]["out_0"]


def _key_head_groups(np_, w):
    n = w.shape[0]
    q, k, v = w[:, :2048].reshape(n, 16, 128), w[:, 2048:4096].reshape(n, 16, 128), w[:, 4096:].reshape(n, 16, 256)
    g = np_.concatenate([q, k, v], axis=2)
    return np_.concatenate([g, g[:, :1]], axis=1).reshape(n, 17 * 512)
```
